# Optimizing a Trainium2 kernel written in Bass

```python
import numpy as np
import jax
import jax.numpy as jnp

def _softmax(x, axis=-1):
    return jax.nn.softmax(x, axis=axis)

def _gelu(x):
    return jax.nn.gelu(x, approximate=True)

def _silu(x):
    return jax.nn.silu(x)

def _sigmoid(x):
    return jax.nn.sigmoid(x)

def _layernorm(x, axis=-1, eps=1e-05):
    m = jnp.mean(x, axis=axis, keepdims=True)
    v = jnp.var(x, axis=axis, keepdims=True)
    return (x - m) / jnp.sqrt(v + eps)

def _scatter_add(tgt, idx, src, axis=0):
    return tgt.at[idx].add(src)

def _segment_sum(src, seg, n):
    return jax.ops.segment_sum(src, seg, n)
kernel_name = 'mk_xattn_ffn_d1_seqx_r4_12fd47'

def setup_inputs(seed: int=0):
    np.random.seed(seed)
    _w = jnp.asarray

    def _rec_inputs():
        import jax
        import jax.numpy as jnp
        _rk = jax.random.key(seed)
        x = 7.22e-05 + 1 * jax.random.normal(jax.random.fold_in(_rk, 1), (8, 256, 512), jnp.float32)
        _lenS = 256 - jax.random.randint(jax.random.fold_in(_rk, 7), (8,), 0, max(1, 256 // 4) + 1, jnp.int32)
        _lenS2 = 256 - jax.random.randint(jax.random.fold_in(_rk, 8), (8,), 0, max(1, 256 // 4) + 1, jnp.int32)
        _ctx_2048P = jax.random.normal(jax.random.fold_in(_rk, 11), (8, 16, 512), jnp.float32)
        _ctx_2048c = jax.random.dirichlet(jax.random.fold_in(_rk, 511), 0.3 * jnp.ones((16,), jnp.float32), (8, 256))
        _ctx_2048t = jnp.einsum('bsk,bkd->bsd', _ctx_2048c, _ctx_2048P)
        _ctx_2048t = _ctx_2048t * jax.lax.rsqrt(jnp.mean(jnp.square(_ctx_2048t)) + 1e-12) * 0.953939
        ctx_2048 = 4.13588e-05 + 0.999923 * (_ctx_2048t + 0.3 * jax.random.normal(jax.random.fold_in(_rk, 611), (8, 256, 512), jnp.float32))
        return (x, ctx_2048)
    x, ctx_2048 = _rec_inputs()

    def _L0_xattn_setup():
        import jax, jax.numpy as jnp
        import numpy as np
        N_HEADS = 16
        K_CH = 256 // N_HEADS
        SCALE = 1.0 / np.sqrt(K_CH)
        key = jax.random.key(seed)
        ks = jax.random.split(key, 10)
        B, C, T = (4, 256, 512)
        Cout = 256
        xavier = lambda k, o, i: jax.random.uniform(k, (o, i), jnp.float32, -1.0, 1.0) * np.sqrt(6.0 / (o + i))
        return {'x': jax.random.normal(ks[0], (B, C, T), jnp.float32), 'c': jax.random.normal(ks[1], (B, C, T), jnp.float32), 'Wq': xavier(ks[2], C, C), 'bq': jnp.zeros((C,), jnp.float32), 'Wk': xavier(ks[3], C, C), 'bk': jnp.zeros((C,), jnp.float32), 'Wv': xavier(ks[4], C, C), 'bv': jnp.zeros((C,), jnp.float32), 'Wo': xavier(ks[5], Cout, C), 'bo': jnp.zeros((Cout,), jnp.float32)}
    _L0_xattn_all = _L0_xattn_setup()
    _L0_xattn_in = {k: v for k, v in _L0_xattn_all.items() if k in ('Wq', 'bq', 'Wk', 'bk', 'Wv', 'bv', 'Wo', 'bo')}
    del _L0_xattn_all

    def _L0_ffn_setup():
        import jax, jax.numpy as jnp
        import numpy as np
        B, S, H = (2, 512, 512)
        FFN = 256
        E = 8
        TOP_K = 2
        key = jax.random.key(seed)
        ks = jax.random.split(key, 5)
        scale = 0.02
        hidden_states = jax.random.normal(ks[0], (B, S, H), dtype=jnp.float32)
        Wg = jax.random.normal(ks[1], (E, H), dtype=jnp.float32) * scale
        W1 = jax.random.normal(ks[2], (E, FFN, H), dtype=jnp.float32) * scale
        W3 = jax.random.normal(ks[3], (E, FFN, H), dtype=jnp.float32) * scale
        W2 = jax.random.normal(ks[4], (E, H, FFN), dtype=jnp.float32) * scale
        bias = jnp.zeros((E,), dtype=jnp.float32)
        return {'hidden_states': hidden_states, 'Wg': Wg, 'W1': W1, 'W2': W2, 'W3': W3, 'bias': bias}
    _L0_ffn_all = _L0_ffn_setup()
    _L0_ffn_in = {k: v for k, v in _L0_ffn_all.items() if k in ('Wg', 'W1', 'W2', 'W3', 'bias')}
    del _L0_ffn_all
    return {'x': x, 'ctx_2048': ctx_2048, 'L0_xattn_Wq': _L0_xattn_in['Wq'], 'L0_xattn_bq': _L0_xattn_in['bq'], 'L0_xattn_Wk': _L0_xattn_in['Wk'], 'L0_xattn_bk': _L0_xattn_in['bk'], 'L0_xattn_Wv': _L0_xattn_in['Wv'], 'L0_xattn_bv': _L0_xattn_in['bv'], 'L0_xattn_Wo': _L0_xattn_in['Wo'], 'L0_xattn_bo': _L0_xattn_in['bo'], 'L0_ffn_Wg': _L0_ffn_in['Wg'], 'L0_ffn_W1': _L0_ffn_in['W1'], 'L0_ffn_W2': _L0_ffn_in['W2'], 'L0_ffn_W3': _L0_ffn_in['W3'], 'L0_ffn_bias': _L0_ffn_in['bias']}

def reference(x, ctx_2048, L0_xattn_Wq, L0_xattn_bq, L0_xattn_Wk, L0_xattn_bk, L0_xattn_Wv, L0_xattn_bv, L0_xattn_Wo, L0_xattn_bo, L0_ffn_Wg, L0_ffn_W1, L0_ffn_W2, L0_ffn_W3, L0_ffn_bias):
    import jax
    import jax.numpy as jnp

    def _L0_xattn_ref(x, c, Wq, bq, Wk, bk, Wv, bv, Wo, bo):
        import jax, jax.numpy as jnp
        import numpy as np
        N_HEADS = 16
        K_CH = 256 // N_HEADS
        SCALE = 1.0 / np.sqrt(K_CH)
        B, C, T = x.shape
        H, K = (N_HEADS, K_CH)
        q = jnp.einsum('oc,bct->bot', Wq, x) + bq[None, :, None]
        k = jnp.einsum('oc,bct->bot', Wk, c) + bk[None, :, None]
        v = jnp.einsum('oc,bct->bot', Wv, c) + bv[None, :, None]
        q = q.reshape(B, H, K, T)
        k = k.reshape(B, H, K, -1)
        v = v.reshape(B, H, K, -1)
        scores = jnp.einsum('bhkt,bhks->bhts', q, k) * SCALE
        p = jax.nn.softmax(scores, axis=-1)
        out = jnp.einsum('bhts,bhks->bhkt', p, v)
        out = out.reshape(B, H * K, T)
        return jnp.einsum('oc,bct->bot', Wo, out) + bo[None, :, None]

    def _L0_ffn_ref(hidden_states, Wg, W1, W2, W3, bias):
        import jax, jax.numpy as jnp
        import numpy as np
        B, S, H = (2, 512, 512)
        FFN = 256
        E = 8
        TOP_K = 2
        bsz, seq_len, hidden_dim = hidden_states.shape
        x = hidden_states.reshape(-1, hidden_dim)
        router_logits = x @ Wg.T
        routing_weights = jax.nn.sigmoid(router_logits.astype(jnp.float32))
        scores = routing_weights + bias
        _, top_k_index = jax.lax.top_k(scores, TOP_K)
        top_k_weights = jnp.take_along_axis(routing_weights, top_k_index, axis=1)
        top_k_weights = top_k_weights / top_k_weights.sum(axis=-1, keepdims=True)
        top_k_weights = top_k_weights.astype(x.dtype)
        one_hot = jax.nn.one_hot(top_k_index, Wg.shape[0], dtype=x.dtype)
        expert_w = jnp.einsum('tk,tke->te', top_k_weights, one_hot)
        h1 = jnp.einsum('th,efh->tef', x, W1)
        h3 = jnp.einsum('th,efh->tef', x, W3)
        g = jax.nn.silu(h1) * h3 * expert_w[:, :, None]
        out = jnp.einsum('tef,ehf->th', g, W2)
        return out.reshape(bsz, seq_len, hidden_dim)
    x = x + _L0_xattn_ref(_layernorm(x, axis=-1), ctx_2048, L0_xattn_Wq, L0_xattn_bq, L0_xattn_Wk, L0_xattn_bk, L0_xattn_Wv, L0_xattn_bv, L0_xattn_Wo, L0_xattn_bo)
    x = x + _L0_ffn_ref(_layernorm(x, axis=-1), L0_ffn_Wg, L0_ffn_W1, L0_ffn_W2, L0_ffn_W3, L0_ffn_bias)
    return x

_drawn_inputs = setup_inputs


def setup_inputs(seed=0):
    import zlib

    import numpy as np

    out = dict(_drawn_inputs(seed))
    spreads = {'L0_xattn_bq': (0.0, 0.1),
     'L0_xattn_bk': (0.0, 0.1),
     'L0_xattn_bv': (0.0, 0.1),
     'L0_xattn_bo': (0.0, 0.1),
     'L0_ffn_bias': (0.0, 0.1)}
    factors = {}
    for name, (base, spread) in spreads.items():
        noise = np.random.default_rng([zlib.crc32(name.encode()), seed]).standard_normal(out[name].shape)
        drawn = base * np.exp(spread * noise) if base else spread * noise
        out[name] = jnp.asarray(drawn.astype(out[name].dtype))
    for name, factor in factors.items():
        out[name] = (out[name] * factor).astype(out[name].dtype)
    return out
```

```python
import concourse.bass as bass
from concourse import mybir
from contextlib import ExitStack

F32 = mybir.dt.float32
F32R = mybir.dt.float32r
BF16 = mybir.dt.bfloat16
U32 = mybir.dt.uint32
ALU = mybir.AluOpType
ACT = mybir.ActivationFunctionType
AX = mybir.AxisListType

P = 128
B, C, T = 8, 256, 512
H, HD = 16, 16
CT = C // P
TT = T // P
UNITS, UH = 4, 4
SLOTS = UH * TT
PARTS = 3
QROWS = 6 * HD
KROWS = QROWS + PARTS
VW = 32
K_GROUPS = ((0, 3), (3, 2), (5, 1))
Q_GROUPS = ((0, 0, 3), (3, 1, 2), (5, 2, 1))
STACK_DMAS = len(K_GROUPS) + len(Q_GROUPS)
LAG = UNITS + 1
SCALE = 1.0 / HD ** 0.5
EPS = 1e-5
E, FF = 8, 256
KT = T // P
FT = FF // P
TILES = B * CT
GT = 4
GROUPS = TILES // GT


def attention(nc, x, ctx_in, wq, bq, wk, bk, wv, bv, wo, bo, x1, q_scratch, o_scratch, r_scratch):
    es = ExitStack()
    with es:
        def sb(name, shape, dt):
            return es.enter_context(nc.sbuf_tensor(name, shape, dt))

        def ps(name, shape):
            return es.enter_context(nc.psum_tensor(name, shape, F32))

        def sem(name):
            return es.enter_context(nc.semaphore(name))

        w_sb = {name: sb(f"{name}_sb", [P, CT, C], F32) for name in ("wq", "wk", "wv", "wo")}
        vecs = sb("vecs", [P, 4, CT], F32)
        bq_sb, bk_sb, bv_sb, bo_sb = (vecs[:, i, :] for i in range(4))
        bout = sb("bout", [P, CT], F32)
        ident = sb("ident", [P, P], F32)
        minus_half = sb("minus_half", [P, CT], F32)
        ctx_sb = sb("ctx_sb", [P, 2, CT, T], F32)
        xn = sb("xn", [P, CT, T], F32)
        stats = sb("stats", [P, CT, 6], F32)
        mean_var = sb("mean_var", [P, CT, 2], F32)
        var_eps = sb("var_eps", [P, CT], F32)
        pace = sb("pace", [P, 1], F32)
        rstd = sb("rstd", [P, CT], F32)
        qk = sb("qk", [P, 2, CT * T], F32)
        parts = sb("parts", [P, 2, PARTS, CT * T], BF16)
        qs = [sb(f"qs{i}", [P, H, T], BF16) for i in range(2)]
        ks = [sb(f"ks{i}", [P, H, T], BF16) for i in range(2)]
        v_sb = [sb(f"v{i}", [P, TT, H, VW], F32) for i in range(2)]
        neg_max = [sb(f"neg_max{i}", [P, H * TT], F32) for i in range(2)]
        m_rest = sb("m_rest", [H * TT, 2, P], F32)
        m_parts = sb("m_parts", [H * TT, PARTS, P], BF16)
        probs = sb("probs", [P, TT, UH, T], F32)
        o_sb = sb("o_sb", [P, 2, T], F32)
        den = sb("den", [P, 64], F32)
        rden = sb("rden", [P, 64], F32)
        o_heads = sb("o_heads", [P, CT, T], F32)
        r_heads = sb("r_heads", [P, CT, T], F32)
        o_norm = sb("o_norm", [P, CT, T], F32)

        st_ps = [ps(f"st_ps{i}", [P, 2, T]) for i in range(2)]
        s_ps = [ps(f"s_ps{i}", [P, T]) for i in range(2)]
        o_ps = ps("o_ps", [P, T])
        misc = ps("misc", [P, T])

        w_loaded = {name: sem(f"{name}_loaded") for name in ("wq", "wk", "wv", "wo")}
        vecs_loaded = sem("vecs_loaded")
        x_loaded = [sem(f"x_loaded{i}") for i in range(2)]
        ctx_loaded = [sem(f"ctx_loaded{i}") for i in range(2)]
        const_ready = sem("const_ready")
        ident_zero = sem("ident_zero")
        ident_ready = sem("ident_ready")
        stats_ready = sem("stats_ready")
        mv_ready = sem("mv_ready")
        eps_added = sem("eps_added")
        rstd_ready = sem("rstd_ready")
        xn_ready = sem("xn_ready")
        qk_ready, qk_done = sem("qk_ready"), sem("qk_done")
        part1, rest1, part2, part3 = sem("part1"), sem("rest1"), sem("part2"), sem("part3")
        parts_stored = [sem(f"parts_stored{i}") for i in range(2)]
        stack_loaded = [sem(f"stack_loaded{u}") for u in range(UNITS)]
        v_ready, v_done = sem("v_ready"), sem("v_done")
        s_ready, max_done = sem("s_ready"), sem("max_done")
        m_ready, m_part1, m_rest1, m_part2, m_rest2, m_done = (
            sem(n) for n in ("m_ready", "m_part1", "m_rest1", "m_part2", "m_rest2", "m_done"))
        m_loaded = sem("m_loaded")
        st_ready, exp_done = sem("st_ready"), sem("exp_done")
        pv_done, o_done = sem("pv_done"), sem("o_done")
        o_stored = [sem(f"o_stored{i}") for i in range(2)]
        den_loaded, rden_ready, rden_stored, heads_loaded = (
            sem(n) for n in ("den_loaded", "rden_ready", "rden_stored", "heads_loaded"))
        on_ready = sem("on_ready")
        wo_ready, wo_done = sem("wo_ready"), sem("wo_done")

        def x1_at(n, ct):
            v = x1[:, bass.ds(n, 1), ct, :]
            return v.rearrange("p o t -> p (o t)")

        def iterate(engine, step):
            for n in (0, 1):
                for u in range(UNITS):
                    step(n, n % 2, u, n // 2)
            with engine.Fori(1, 3) as i:
                for par in range(2):
                    for u in range(UNITS):
                        step(2 * i + par, par, u, i)
            for n in (6, 7, 8, 9):
                for u in range(UNITS):
                    step(n, n % 2, u, n // 2)

        def late(n, first):
            return n >= first if isinstance(n, int) else 2 >= first

        def early(n, last):
            return n <= last if isinstance(n, int) else 5 <= last

        def unit_runs(n, u):
            return not isinstance(n, int) or 0 <= UNITS * n + u - LAG < UNITS * B

        block = es.enter_context(nc.Block())


        @block.sync
        def _(sp):
            def load_x(m, par):
                sp.dma_start(x1[:, bass.ds(m, 1), :, :].rearrange("p o c t -> p (o c) t"),
                             x[bass.ds(m, 1)].rearrange("o (c p) t -> p (o c) t", p=P)).then_inc(x_loaded[par], 16)

            def load_ctx(m, par):
                sp.dma_start(ctx_sb[:, par, :, :],
                             ctx_in[bass.ds(m, 1)].rearrange("o (c p) t -> p (o c) t", p=P)).then_inc(ctx_loaded[par], 16)

            def store_parts(m, par):
                sp.wait_ge(part3, m + 1)
                sp.dma_start(q_scratch[bass.ds(m, 1)].rearrange("o w g (c k) h t -> (k h) (o w g c) t", c=CT),
                             parts[:, :, :, :].rearrange("p w g (c t) -> p (w g c) t", c=CT)
                             ).then_inc(parts_stored[par], 16)

            rows = q_scratch.rearrange("n w g k h t -> n w (g k) h t")

            def load_stack(m, par, i, u):
                if late(m, 2):
                    sp.wait_ge(pv_done, UNITS * TT * (m - 2) + TT * (u + 1))
                if u == 0:
                    sp.wait_ge(parts_stored[par], 16 * i + 16)
                heads = slice(UH * u, UH * (u + 1))

                for g, count in K_GROUPS:
                    src = rows[bass.ds(m, 1), 1, 0:HD * count, heads, :]
                    sp.dma_start(ks[par][HD * g:HD * (g + count), heads, :],
                                 src.rearrange("o r h t -> (o r) h t")).then_inc(stack_loaded[u], 16)
                for g, part, count in Q_GROUPS:
                    src = rows[bass.ds(m, 1), 0, HD * part:HD * (part + 1), heads, :]
                    sp.dma_start(qs[par][HD * g:HD * (g + count), heads, :],
                                 src.rearrange("o r h t -> o r (h t)").to_broadcast([count, HD, UH * T])
                                 ).then_inc(stack_loaded[u], 16)

            def load_m_rows(m, par):
                sp.wait_ge(m_done, m + 1)
                for g in range(PARTS):
                    sp.dma_start(qs[par][QROWS + g:QROWS + g + 1, :, :].rearrange("o h (a t) -> o (h a) t", a=TT),
                                 m_parts[:, g, :]).then_inc(m_loaded, 16)

            def store_o(n, u):
                tc = UNITS * n + u - LAG - 1
                m, mu = (n - 1, u - 2) if u >= 2 else (n - 2, u + 2)
                sp.wait_ge(o_done, tc + 1)
                sp.dma_start(o_scratch[bass.ds(m, 1), mu].rearrange("o r t -> (o r) t"),
                             o_sb[:, mu % 2, :]).then_inc(o_stored[mu % 2], 16)

            def load_den(m):
                for i in range(2):
                    sp.wait_ge(o_stored[i], 32 * (m + 1))
                den_rows = o_scratch.rearrange("n u (j r) t -> n (u j) r t", r=VW)
                sp.dma_start(den[:, :], den_rows[bass.ds(m, 1), :, HD, :].rearrange("o h t -> (o h) t")
                             ).then_inc(den_loaded, 16)
                for ct in range(CT):
                    src = den_rows[bass.ds(m, 1), 8 * ct:8 * (ct + 1), 0:HD, :]
                    sp.dma_start(o_heads[:, ct, :], src.rearrange("o h r t -> (o h) r t")).then_inc(heads_loaded, 16)
                sp.wait_ge(rden_ready, m + 1)
                sp.dma_start(r_scratch[bass.ds(m, 1)].rearrange("o h (a t) -> (o h a) t", a=8),
                             rden[:, :]).then_inc(rden_stored, 16)
                sp.wait_ge(rden_stored, 16 * (m + 1))
                for ct in range(CT):
                    src = r_scratch[bass.ds(m, 1), 8 * ct:8 * (ct + 1), :].rearrange("o (h r) t -> (o h) r t", r=1)
                    sp.dma_start(r_heads[:, ct, :], src.to_broadcast([8, HD, T])).then_inc(heads_loaded, 16)

            for name, src in (("wq", wq), ("wk", wk), ("wv", wv), ("wo", wo)):
                sp.dma_start(w_sb[name][:, :, :], src.rearrange("(c p) o -> p c o", p=P)).then_inc(w_loaded[name], 16)
                if name == "wq":
                    load_x(0, 0)
                    load_ctx(0, 0)
                    for vec, v in enumerate((bq, bk, bv, bo)):
                        sp.dma_start(vecs[:, vec, :], v.rearrange("p c -> p c")).then_inc(vecs_loaded, 16)
            load_x(1, 1)
            load_ctx(1, 1)
            store_parts(0, 0)
            load_stack(0, 0, 0, 0)
            load_stack(0, 0, 0, 1)

            def step(n, par, u, i):
                if unit_runs(n, u - 1) and u >= 0:
                    store_o(n, u)
                if u == 0 and early(n, 5):
                    load_x(n + 2, par)
                if u == 2 and early(n, 6):
                    load_stack(n + 1, 1 - par, i + par, 0)
                if u == 3 and early(n, 6):
                    load_stack(n + 1, 1 - par, i + par, 1)
                if u == 0 and early(n, 7):
                    load_stack(n, par, i, 2)
                if u == 1 and early(n, 7):
                    load_stack(n, par, i, 3)
                if u == 1 and late(n, 2):
                    load_den(n - 2)
                if u == 1 and early(n, 6):
                    store_parts(n + 1, 1 - par)
                if u == 0 and late(n, 1) and early(n, 8):
                    load_m_rows(n - 1, 1 - par)
                if u == 3 and early(n, 5):
                    sp.wait_ge(v_ready, 2 * (n + 1))
                    load_ctx(n + 2, par)

            iterate(sp, step)

        @block.gpsimd
        def _(pool):
            nc.gpsimd.memset(minus_half[:, :], -0.5)
            nc.gpsimd.memset(ident[:, :], 0.0).then_inc(ident_zero, 1)
            pool.wait_ge(ident_zero, 1)
            nc.gpsimd.affine_select(out=ident[:, :], in_=ident[:, :], compare_op=ALU.not_equal, fill=1.0, base=0,
                                    pattern=[[-1, P]], channel_multiplier=1).then_inc(ident_ready, 1)
            for buf in v_sb:
                nc.gpsimd.memset(buf[:, :, :, HD:VW], 1.0).then_inc(const_ready, 1)

            def norm_scale(m):
                pool.wait_ge(eps_added, m + 1)
                nc.gpsimd.tensor_tensor(rstd[:, :], var_eps[:, :], minus_half[:, :], ALU.pow).then_inc(rstd_ready, 1)

            def split(m):
                pool.wait_ge(part1, m + 1)
                nc.gpsimd.tensor_tensor(qk[:, :, :], qk[:, :, :], parts[:, :, 0, :], ALU.subtract).then_inc(rest1, 1)
                pool.wait_ge(part2, m + 1)
                nc.gpsimd.tensor_tensor(parts[:, :, 2, :], qk[:, :, :], parts[:, :, 1, :],
                                        ALU.subtract).then_inc(part3, 1)

            def normalize(m):
                pool.wait_ge(heads_loaded, 2 * CT * 16 * (m + 1))
                pool.wait_ge(wo_ready, CT * m + 1)
                nc.gpsimd.tensor_tensor(o_norm[:, :, :], o_heads[:, :, :], r_heads[:, :, :],
                                        ALU.mult).then_inc(on_ready, 1)

            norm_scale(0)
            norm_scale(1)
            split(0)

            def step(n, par, u, i):
                if u == 1 and early(n, 6):
                    split(n + 1)
                if u == 2 and late(n, 2):
                    normalize(n - 2)
                if u == 3 and early(n, 5):
                    norm_scale(n + 2)

            iterate(pool, step)

        @block.scalar
        def _(act):
            def evacuate_qk(m, j):
                act.wait_ge(qk_ready, 4 * m + j + 1)
                if j == 0 and late(m, 1):
                    act.wait_ge(part3, m)
                bias = (bq_sb, bk_sb)[j // CT][:, j % CT:j % CT + 1]
                nc.scalar.activation(qk[:, j // CT, T * (j % CT):T * (j % CT + 1)], misc[:, :], ACT.Identity,
                                     bias=bias).then_inc(qk_done, 1)

            def evacuate_v(m, par, j):
                act.wait_ge(v_ready, 2 * m + j + 1)
                if j == 0 and late(m, 2):
                    act.wait_ge(pv_done, UNITS * TT * (m - 1))
                nc.scalar.copy(v_sb[par][:, 2 * j:2 * j + 2, :, 0:HD],
                               misc[:, :].rearrange("p (s h k) -> p s h k", s=2, h=H)).then_inc(v_done, 1)

            def evacuate_o(tc, n, u):
                act.wait_ge(pv_done, TT * (tc + 1))
                if late(tc, 2):
                    act.wait_ge(o_stored[u % 2], 16 * (2 * n + (u - 6) // 2))
                nc.scalar.copy(o_sb[:, u % 2, :], o_ps[:, :]).then_inc(o_done, 1)

            act.wait_ge(vecs_loaded, 4 * 16)
            for j in range(2 * CT):
                evacuate_qk(0, j)

            def step(n, par, u, i):
                tc = UNITS * n + u - LAG
                for pair in range(SLOTS // 2):
                    if unit_runs(n, u):
                        g = (SLOTS // 2) * tc + pair
                        act.wait_ge(st_ready, g + 1)
                        if pair % 2 == 0 and late(tc, 1):
                            act.wait_ge(pv_done, TT * (tc - 1) + pair // 2 + 1)
                        half = 2 * (pair % 2)
                        nc.scalar.activation(probs[:, pair // 2, half:half + 2, :], st_ps[pair % 2][:, :, :], ACT.Exp,
                                             scale=SCALE).then_inc(exp_done, 1)
                    if pair == 2 and unit_runs(n, u - 1):
                        evacuate_o(tc - 1, n, u)
                    if early(n, 6) and u == 0 and pair in (2, 4, 6):
                        evacuate_qk(n + 1, pair // 2 - 1)
                    if early(n, 6) and u == 1 and pair == 2:
                        evacuate_qk(n + 1, 3)
                    if early(n, 7) and u == 2 and pair in (2, 5):
                        evacuate_v(n, par, pair // 4)

            iterate(act, step)

        @block.vector
        def _(dve):
            def norm_stats(m, par, i):
                dve.wait_ge(x_loaded[par], 16 * i + 16)
                for ct in range(CT):
                    nc.vector.bn_stats(stats[:, ct, :], x1_at(m, ct)).then_inc(stats_ready, 1)
                dve.wait_ge(stats_ready, CT * (m + 1))
                nc.vector.memset(pace[:, :], 0.0)
                for ct in range(CT):
                    nc.vector.bn_aggr(mean_var[:, ct, :], stats[:, ct, :]).then_inc(mv_ready, 1)
                dve.wait_ge(mv_ready, CT * (m + 1))
                nc.vector.tensor_scalar(var_eps[:, :], mean_var[:, :, 1], EPS, None, ALU.add).then_inc(eps_added, 1)

            def norm_apply(m):
                dve.wait_ge(rstd_ready, m + 1)
                if late(m, 1):
                    dve.wait_ge(qk_ready, 4 * (m - 1) + CT)
                for ct in range(CT):
                    nc.vector.tensor_scalar(xn[:, ct, :], x1_at(m, ct), mean_var[:, ct, 0:1], rstd[:, ct:ct + 1],
                                            ALU.subtract, ALU.mult).then_inc(xn_ready, 1)

            def round_first(m, par, i):
                dve.wait_ge(qk_done, 4 * (m + 1))
                if late(m, 1):
                    dve.wait_ge(parts_stored[1 - par], 16 * (i + par))
                nc.vector.tensor_copy(parts[:, :, 0, :], qk[:, :, :]).then_inc(part1, 1)

            def round_second(m):
                dve.wait_ge(rest1, m + 1)
                nc.vector.tensor_copy(parts[:, :, 1, :], qk[:, :, :]).then_inc(part2, 1)

            def split_max(m):
                dve.wait_ge(m_ready, m + 1)
                if late(m, 1):
                    dve.wait_ge(m_loaded, 16 * PARTS * m)
                mt = misc[0:H * TT, 0:P]
                nc.vector.tensor_copy(m_parts[:, 0, :], mt).then_inc(m_part1, 1)
                dve.wait_ge(m_part1, m + 1)
                nc.vector.tensor_tensor(m_rest[:, 0, :], mt, m_parts[:, 0, :], ALU.subtract).then_inc(m_rest1, 1)
                dve.wait_ge(m_rest1, m + 1)
                nc.vector.tensor_copy(m_parts[:, 1, :], m_rest[:, 0, :]).then_inc(m_part2, 1)
                dve.wait_ge(m_part2, m + 1)
                nc.vector.tensor_tensor(m_parts[:, 2, :], m_rest[:, 0, :], m_parts[:, 1, :],
                                        ALU.subtract).then_inc(m_done, 1)

            def add_residual(m, ot):
                dve.wait_ge(wo_ready, 1 + CT * m + ot + 1)
                nc.vector.scalar_tensor_tensor(out=x1_at(m, ot), in0=misc[:, :], scalar=bout[:, ot:ot + 1],
                                               in1=x1_at(m, ot), op0=ALU.add, op1=ALU.add).then_inc(wo_done, 1)

            for buf in ks:
                nc.vector.memset(buf[QROWS:KROWS, :, :], 1.0).then_inc(const_ready, 1)
            dve.wait_ge(vecs_loaded, 4 * 16)
            dve.wait_ge(wo_ready, 1)
            nc.vector.tensor_tensor(bout[:, :], misc[:, 0:CT], bo_sb, ALU.add).then_inc(wo_done, 1)
            norm_stats(0, 0, 0)
            norm_apply(0)
            norm_stats(1, 1, 0)
            norm_apply(1)
            round_first(0, 0, 0)
            round_second(0)

            def step(n, par, u, i):
                if early(n, 7) and u == 0 and late(n, 2):
                    dve.wait_ge(m_ready, n - 1)
                for slot in range(SLOTS):
                    if early(n, 7):
                        dve.wait_ge(s_ready, SLOTS * (UNITS * n + u) + slot + 1)
                        col = SLOTS * u + slot
                        nc.vector.tensor_reduce(neg_max[par][:, col:col + 1], s_ps[slot % 2][:, :], AX.X, ALU.max,
                                                negate=True).then_inc(max_done, 1)
                    if u == 0 and slot == 3 and late(n, 1) and early(n, 8):
                        split_max(n - 1)
                    if u == 1 and early(n, 6):
                        if slot == 7:
                            round_first(n + 1, 1 - par, i + par)
                        if slot == 13:
                            round_second(n + 1)
                    if u == 2 and slot == 0 and late(n, 2):
                        dve.wait_ge(den_loaded, 16 * (n - 1))
                        nc.vector.reciprocal(rden[:, :], den[:, :]).then_inc(rden_ready, 1)
                    if u == 3 and early(n, 5):
                        if slot == 1:
                            norm_stats(n + 2, par, i + 1)
                        if slot == 4:
                            norm_apply(n + 2)
                    if u == 3 and slot in (7, 13) and late(n, 2):
                        add_residual(n - 2, slot // 13)

            iterate(dve, step)

        @block.tensor
        def _(pe):
            def project_qk(m, par, i, j):
                which, ct_out = j // CT, j % CT
                w, src = (w_sb["wq"], xn) if which == 0 else (w_sb["wk"], ctx_sb[:, par])
                if j == 0:
                    pe.wait_ge(xn_ready, CT * (m + 1))
                    if late(m, 1):
                        pe.wait_ge(qk_done, 4 * m)
                    if late(m, 2):
                        pe.wait_ge(m_rest1, m - 1)
                if j == CT:
                    pe.wait_ge(ctx_loaded[par], 16 * i + 16)
                if j:
                    pe.wait_ge(qk_done, 4 * m + j)
                for ct in range(CT):
                    last = nc.tensor.matmul(misc[:, :], w[:, ct, P * ct_out:P * (ct_out + 1)], src[:, ct, :],
                                            start=(ct == 0), stop=(ct == CT - 1))
                last.then_inc(qk_ready, 1)

            def project_v(m, par, j):
                if j == 0:
                    if early(m, 6):
                        pe.wait_ge(qk_done, 4 * (m + 2))
                    else:
                        pe.wait_ge(m_rest1, m)
                else:
                    pe.wait_ge(v_done, 2 * m + 1)
                for half in range(2):
                    s0 = P * (2 * j + half)
                    for ct in range(CT):
                        last = nc.tensor.matmul(misc[:, C * half:C * (half + 1)], ctx_sb[:, par, ct, s0:s0 + P],
                                                w_sb["wv"][:, ct, :], start=(ct == 0), stop=(ct == CT - 1))
                last.then_inc(v_ready, 1)

            def project_out(m, ot):
                if ot == 0:
                    pe.wait_ge(on_ready, m + 1)
                    if early(m, 5):
                        pe.wait_ge(v_done, 2 * (m + 3))
                    else:
                        pe.wait_ge(m_rest1, B)
                pe.wait_ge(wo_done, 1 + CT * m + ot)
                for ct in range(CT):
                    last = nc.tensor.matmul(misc[:, :], w_sb["wo"][:, ct, P * ot:P * (ot + 1)], o_norm[:, ct, :],
                                            start=(ct == 0), stop=(ct == CT - 1))
                last.then_inc(wo_ready, 1)

            def wait_to_transpose(m):
                pe.wait_ge(max_done, UNITS * SLOTS * (m + 1))
                pe.wait_ge(v_done, 2 * (m + 1))
                if late(m, 2):
                    pe.wait_ge(wo_done, 1 + CT * (m - 1))

            def transpose_max(par):
                nc.tensor.transpose(misc[0:H * TT, 0:P], neg_max[par][:, :], ident[:, :]).then_inc(m_ready, 1)

            def weigh_values(tc, u, par, st):
                pe.wait_ge(exp_done, (SLOTS // 2) * tc + 2 * (st + 1))
                if st == 0 and late(tc, 1):
                    pe.wait_ge(o_done, tc)
                for j in range(UH):
                    last = nc.tensor.matmul(o_ps[VW * j:VW * (j + 1), :], v_sb[par][:, st, UH * u + j, :],
                                            probs[:, st, j, :], start=(st == 0), stop=(st == TT - 1),
                                            skip_group_check=True)
                last.then_inc(pv_done, 1)

            for name in ("wo", "wv"):
                pe.wait_ge(w_loaded[name], 16)
            pe.wait_ge(vecs_loaded, 4 * 16)
            for ot in range(CT):
                for ct in range(CT):
                    last = nc.tensor.matmul(misc[:, ot:ot + 1], w_sb["wo"][:, ct, P * ot:P * (ot + 1)],
                                            bv_sb[:, ct:ct + 1], start=(ct == 0), stop=(ct == CT - 1))
            last.then_inc(wo_ready, 1)
            for name in ("wq", "wk"):
                pe.wait_ge(w_loaded[name], 16)
            pe.wait_ge(ident_ready, 1)
            pe.wait_ge(const_ready, 4)
            pe.wait_ge(wo_done, 1)
            for j in range(2 * CT):
                project_qk(0, 0, 0, j)

            def step(n, par, u, i):
                tc = UNITS * n + u - LAG
                cu, cpar = (u - 1, 1 - par) if u else (UNITS - 1, par)
                if early(n, 7):
                    pe.wait_ge(stack_loaded[u], 16 * STACK_DMAS * (n + 1))
                if u == 1 and unit_runs(n, u):
                    pe.wait_ge(m_loaded, 16 * PARTS * n)
                    pe.wait_ge(v_done, 2 * n)
                for slot in range(SLOTS):
                    turns = u == 0 and slot == 2 and late(n, 1) and early(n, 8)
                    if turns:
                        wait_to_transpose(n - 1)
                    if early(n, 7):
                        g = SLOTS * (UNITS * n + u) + slot
                        if slot >= 2 or u >= 1 or late(n, 1):
                            pe.wait_ge(max_done, g - 1)
                        h, tt = UH * u + slot // TT, slot % TT
                        nc.tensor.matmul(s_ps[slot % 2][:, :], qs[par][0:QROWS, h, P * tt:P * (tt + 1)],
                                         ks[par][0:QROWS, h, :], start=True, stop=True).then_inc(s_ready, 1)
                    if unit_runs(n, u):
                        pair, half = slot // 2, slot % 2
                        if half == 0 and (pair >= 2 or late(tc, 1)):
                            pe.wait_ge(exp_done, (SLOTS // 2) * tc + pair - 1)
                        st, h = slot // UH, UH * cu + slot % UH
                        last = nc.tensor.matmul(st_ps[pair % 2][:, half, :], ks[cpar][0:KROWS, h, P * st:P * (st + 1)],
                                                qs[cpar][0:KROWS, h, :], start=True, stop=True)
                        if half == 1:
                            last.then_inc(st_ready, 1)
                    if slot == 3 and unit_runs(n, u - 1):
                        pu, ppar = (cu - 1, cpar) if cu else (UNITS - 1, 1 - cpar)
                        weigh_values(tc - 1, pu, ppar, TT - 1)
                    if slot % UH == UH - 1 and slot > UH and unit_runs(n, u):
                        weigh_values(tc, cu, cpar, slot // UH - 1)
                    if turns:
                        transpose_max(1 - par)
                    if early(n, 6) and u == 0 and slot in (4, 8, 12):
                        project_qk(n + 1, 1 - par, i + par, slot // 4 - 1)
                    if early(n, 6) and u == 1 and slot == 4:
                        project_qk(n + 1, 1 - par, i + par, 3)
                    if early(n, 7) and u == 2 and slot in (4, 10):
                        project_v(n, par, slot // 10)
                    if late(n, 2) and u == 3 and slot in (6, 12):
                        project_out(n - 2, slot // 12)

            iterate(pe, step)


def experts(nc, x1, wg, w1, w3, w2, bias, out):
    es = ExitStack()
    with es:
        def sb(name, shape, dt):
            return es.enter_context(nc.sbuf_tensor(name, shape, dt))

        def ps(name, shape):
            return es.enter_context(nc.psum_tensor(name, shape, F32))

        def sem(name):
            return es.enter_context(nc.semaphore(name))

        xt_hi = sb("xt_hi", [P, KT, TILES * P], F32R)
        xt_lo = sb("xt_lo", [P, KT, TILES * P], F32R)
        w13_raw = sb("w13_raw", [P, KT, 2 * FF], F32)
        w2_raw = sb("w2_raw", [P, FT, T], F32)
        w13_hi = [sb(f"w13_hi{i}", [P, KT, 2 * FF], F32R) for i in range(2)]
        w13_lo = [sb(f"w13_lo{i}", [P, KT, 2 * FF], F32R) for i in range(2)]
        w2_hi = [sb(f"w2_hi{i}", [P, FT, T], F32R) for i in range(2)]
        w2_lo = [sb(f"w2_lo{i}", [P, FT, T], F32R) for i in range(2)]
        silu = sb("silu", [P, FT, T], F32)
        g_hi = [sb(f"g_hi{i}", [P, FT, T], F32R) for i in range(2)]
        g_lo = [sb(f"g_lo{i}", [P, FT, T], F32R) for i in range(2)]
        g_full = sb("g_full", [P, FT, T], F32)
        ident = sb("ident2", [P, P], F32)
        minus_half = sb("minus_half2", [P, GT], F32)
        stats = sb("stats2", [P, GT, 6], F32)
        mean_var = sb("mean_var2", [P, GT, 2], F32)
        var_eps = sb("var_eps2", [P, GT], F32)
        pace = sb("pace2", [P, 1], F32)
        rstd = sb("rstd2", [P, GT], F32)
        xn = [silu[:, i, :] for i in range(2)]
        wg_raw = sb("wg_raw", [P, KT, E], F32)
        wg_hi = sb("wg_hi", [P, KT, P], F32R)
        wg_lo = sb("wg_lo", [P, KT, P], F32R)
        logits_t = sb("logits_t", [P, T], F32)
        logits = sb("logits", [P, TILES, E], F32)
        bias_row = sb("bias_row", [P, E], F32)
        lanes = sb("lanes", [P, E], F32)
        route = sb("route", [P, TILES, E], F32)
        score = sb("score", [P, TILES, E], F32)
        top = sb("top", [P, TILES, E], F32)
        top_at = sb("top_at", [P, TILES, E], U32)
        top_atf = sb("top_atf", [P, TILES, 2], F32)
        first = sb("first", [P, TILES, E], F32)
        second = sb("second", [P, TILES, E], F32)
        total = sb("total", [P, TILES], F32)
        rtotal = sb("rtotal", [P, TILES], F32)
        weight = sb("weight", [P, TILES, E], F32)

        h_ps = ps("h_ps", [P, 2, FT, T])
        y_ps = ps("y_ps", [P, GT, T])

        route_loaded, raw_loaded, raw_split = sem("route_loaded"), sem("raw_loaded"), sem("raw_split")
        hi_split = sem("hi_split")
        zeroed, consts, ident_zero = sem("zeroed"), sem("consts"), sem("ident_zero2")
        wg_hi_ready, wg_lo_ready = sem("wg_hi_ready"), sem("wg_lo_ready")
        stats_ready, mv_ready, eps_added, rstd_ready = (
            sem(n) for n in ("stats_ready2", "mv_ready2", "eps_added2", "rstd_ready2"))
        xn_ready, xt_ready, hi_done, lo_done = sem("xn_ready2"), sem("xt_ready"), sem("hi_done"), sem("lo_done")
        logits_ready, logits_done, lt_ready, lt_done = (
            sem(n) for n in ("logits_ready", "logits_done", "lt_ready", "lt_done"))
        routed, chain = sem("routed"), sem("chain")
        h_ready, silu_done, g_done, g_hi_done, g_lo_done = (
            sem(n) for n in ("h_ready", "silu_done", "g_done", "g_hi_done", "g_lo_done"))
        y_ready, added, stored = sem("y_ready"), sem("added"), sem("stored")

        tiles = x1[:, :, :, :].rearrange("p n c t -> p (n c) t")
        out_tiles = out.rearrange("n (c p) t -> p (n c) t", p=P)

        def tile_at(i):
            return tiles[:, bass.ds(i, 1), :].rearrange("p o t -> p (o t)")

        def f32(ap):
            return ap.bitcast(F32)

        PAIRS = E // 2

        def over_pairs(engine, pair):
            pair(0, True, False)
            with engine.Fori(1, PAIRS - 1) as i:
                pair(i, False, False)
            pair(PAIRS - 1, False, True)

        block = es.enter_context(nc.Block())

        @block.sync
        def _(sp):
            sp.dma_start(wg_raw[:, :, :], wg.rearrange("(k p) e -> p k e", p=P)).then_inc(route_loaded, 16)
            sp.dma_start(bias_row[:, :], bias.to_broadcast([P, E])).then_inc(route_loaded, 16)

            def load(e):
                sp.dma_start(w13_raw[:, :, 0:FF], w1[bass.ds(e, 1)].rearrange("o (k p) f -> p (o k) f", p=P)
                             ).then_inc(raw_loaded, 16)
                sp.dma_start(w13_raw[:, :, FF:2 * FF], w3[bass.ds(e, 1)].rearrange("o (k p) f -> p (o k) f", p=P)
                             ).then_inc(raw_loaded, 16)
                sp.dma_start(w2_raw[:, :, :], w2[bass.ds(e, 1)].rearrange("o (k p) t -> p (o k) t", p=P)
                             ).then_inc(raw_loaded, 16)

            load(0)
            with sp.Fori(1, E) as e:
                sp.wait_ge(raw_split, e)
                load(e)
            for i in range(TILES):
                sp.wait_ge(added, TILES * (E - 1) + i + 1)
                sp.dma_start(out_tiles[:, i, :], tiles[:, i, :]).then_inc(stored, 16)
            sp.wait_ge(stored, 16 * TILES)

        @block.gpsimd
        def _(pool):
            nc.gpsimd.memset(minus_half[:, :], -0.5)
            nc.gpsimd.memset(ident[:, :], 0.0).then_inc(ident_zero, 1)
            pool.wait_ge(ident_zero, 1)
            nc.gpsimd.affine_select(out=ident[:, :], in_=ident[:, :], compare_op=ALU.not_equal, fill=1.0, base=0,
                                    pattern=[[-1, P]], channel_multiplier=1).then_inc(consts, 1)
            nc.gpsimd.iota(lanes[:, :], pattern=[[1, E]], base=0, channel_multiplier=0,
                           allow_small_or_imprecise_dtypes=True).then_inc(consts, 1)
            with pool.Fori(0, GROUPS) as g:
                pool.wait_ge(eps_added, g + 1)
                nc.gpsimd.tensor_tensor(rstd[:, :], var_eps[:, :], minus_half[:, :], ALU.pow).then_inc(rstd_ready, 1)

            def cut(e, par, is_first):
                pool.wait_ge(hi_split, e + 1)
                nc.gpsimd.tensor_tensor(w13_lo[par][:, :, :], w13_raw[:, :, :], f32(w13_hi[par][:, :, :]), ALU.subtract)
                nc.gpsimd.tensor_tensor(w2_lo[par][:, :, :], w2_raw[:, :, :], f32(w2_hi[par][:, :, :]),
                                        ALU.subtract).then_inc(raw_split, 1)

            def pair(i, is_first, is_last):
                for par in range(2):
                    e = 2 * i + par
                    for tg in range(GROUPS):
                        g = GROUPS * e + tg
                        for ft in range(FT):
                            pool.wait_ge(g_hi_done, FT * g + ft + 1)
                            nc.gpsimd.tensor_tensor(g_lo[tg % 2][:, ft, :], g_full[:, ft, :],
                                                    f32(g_hi[tg % 2][:, ft, :]), ALU.subtract).then_inc(g_lo_done, 1)
                        if tg == 1 and not (is_last and par == 1):
                            cut(e + 1, 1 - par, False)

            cut(0, 0, True)
            over_pairs(pool, pair)

        @block.scalar
        def _(act):
            act.wait_ge(route_loaded, 32)
            act.wait_ge(zeroed, 2)
            nc.scalar.copy(wg_hi[:, :, 0:E], wg_raw[:, :, :]).then_inc(wg_hi_ready, 1)

            def cut(e, par, is_first):
                act.wait_ge(raw_loaded, 48 * (e + 1))
                nc.scalar.copy(w13_hi[par][:, :, :], w13_raw[:, :, :])
                nc.scalar.copy(w2_hi[par][:, :, :], w2_raw[:, :, :]).then_inc(hi_split, 1)

            with act.Fori(0, GROUPS) as g:
                for tl in range(GT):
                    act.wait_ge(xt_ready, GT * g + tl + 1)
                    nc.scalar.copy(xt_hi[:, :, bass.ds(T * g + P * tl, P)],
                                   h_ps[:, 0, tl % 2, :].rearrange("p (k t) -> p k t", k=KT)).then_inc(hi_done, 1)
                act.wait_ge(logits_ready, g + 1)
                nc.scalar.copy(logits_t[:, :], y_ps[:, 0, :]).then_inc(logits_done, 1)
            act.wait_ge(lt_done, GROUPS)
            nc.scalar.activation(route[:, :, :], logits[:, :, :], ACT.Sigmoid).then_inc(routed, 1)
            cut(0, 0, True)

            def pair(i, is_first, is_last):
                for par in range(2):
                    e = 2 * i + par
                    for tg in range(GROUPS):
                        g = GROUPS * e + tg
                        started = not (is_first and par == 0 and tg == 0)
                        for ft in range(FT):
                            act.wait_ge(h_ready, FT * g + ft + 1)
                            if started:
                                act.wait_ge(g_done, FT * (g - 1) + ft + 1)
                            nc.scalar.activation(silu[:, ft, :], h_ps[:, 0, ft, :], ACT.Silu).then_inc(silu_done, 1)
                        for ft in range(FT):
                            act.wait_ge(g_done, FT * g + ft + 1)
                            if ft == 0 and not (is_first and par == 0 and tg < 2):
                                act.wait_ge(y_ready, GT * (g - 1))
                            nc.scalar.copy(g_hi[tg % 2][:, ft, :], g_full[:, ft, :]).then_inc(g_hi_done, 1)
                        if tg == 0 and not (is_last and par == 1):
                            if started:
                                act.wait_ge(y_ready, GT * g)
                            cut(e + 1, 1 - par, False)

            over_pairs(act, pair)

        @block.vector
        def _(dve):
            def subtract_hi(g, tl):
                dve.wait_ge(hi_done, GT * g + tl + 1)
                cols = bass.ds(T * g + P * tl, P)
                nc.vector.tensor_tensor(xt_lo[:, :, cols], h_ps[:, 0, tl % 2, :].rearrange("p (k t) -> p k t", k=KT),
                                        f32(xt_hi[:, :, cols]), ALU.subtract).then_inc(lo_done, 1)

            nc.vector.memset(wg_hi[:, :, :].bitcast(F32), 0.0).then_inc(zeroed, 1)
            nc.vector.memset(wg_lo[:, :, :].bitcast(F32), 0.0).then_inc(zeroed, 1)
            dve.wait_ge(wg_hi_ready, 1)
            nc.vector.tensor_tensor(wg_lo[:, :, 0:E], wg_raw[:, :, :], f32(wg_hi[:, :, 0:E]),
                                    ALU.subtract).then_inc(wg_lo_ready, 1)
            with dve.Fori(0, GROUPS) as g:
                for tl in range(GT):
                    nc.vector.bn_stats(stats[:, tl, :], tile_at(GT * g + tl)).then_inc(stats_ready, 1)
                dve.wait_ge(stats_ready, GT * g + GT)
                nc.vector.memset(pace[:, :], 0.0)
                for tl in range(GT):
                    nc.vector.bn_aggr(mean_var[:, tl, :], stats[:, tl, :]).then_inc(mv_ready, 1)
                dve.wait_ge(mv_ready, GT * g + GT)
                nc.vector.tensor_scalar(var_eps[:, :], mean_var[:, :, 1], EPS, None, ALU.add).then_inc(eps_added, 1)
                dve.wait_ge(rstd_ready, g + 1)
                for tl in range(GT):
                    nc.vector.tensor_scalar(xn[tl % 2], tile_at(GT * g + tl), mean_var[:, tl, 0:1], rstd[:, tl:tl + 1],
                                            ALU.subtract, ALU.mult).then_inc(xn_ready, 1)
                    if tl:
                        subtract_hi(g, tl - 1)
                subtract_hi(g, GT - 1)
                dve.wait_ge(lt_ready, g + 1)
                nc.vector.tensor_copy(logits[:, bass.ds(GT * g, GT), :],
                                      y_ps[:, 1, :].rearrange("p (a e) -> p a e", a=GT)[:, :, 0:E]).then_inc(lt_done, 1)
            count = [0]

            def link(instruction):
                count[0] += 1
                instruction.then_inc(chain, 1)
                dve.wait_ge(chain, count[0])

            dve.wait_ge(routed, 1)
            dve.wait_ge(consts, 2)
            every = [P, TILES, E]
            link(nc.vector.tensor_tensor(score[:, :, :], route[:, :, :],
                                         bias_row[:, :].rearrange("p (o e) -> p o e", o=1).to_broadcast(every), ALU.add))
            for i in range(TILES):
                link(nc.vector.max(top[:, i, :], score[:, i, :]))
                link(nc.vector.max_index(top_at[:, i, :], top[:, i, :], score[:, i, :]))
            link(nc.vector.tensor_copy(top_atf[:, :, :], top_at[:, :, 0:2]))
            lane = lanes[:, :].rearrange("p (o e) -> p o e", o=1).to_broadcast(every)
            link(nc.vector.tensor_tensor(first[:, :, :], lane, top_atf[:, :, 0:1].to_broadcast(every), ALU.is_equal))
            link(nc.vector.tensor_tensor(second[:, :, :], lane, top_atf[:, :, 1:2].to_broadcast(every), ALU.is_equal))
            link(nc.vector.tensor_tensor(first[:, :, :], first[:, :, :], second[:, :, :], ALU.add))
            link(nc.vector.tensor_tensor(first[:, :, :], first[:, :, :], route[:, :, :], ALU.mult))
            link(nc.vector.tensor_reduce(total[:, :], first[:, :, :], AX.X, ALU.add))
            link(nc.vector.reciprocal(rtotal[:, :], total[:, :]))
            link(nc.vector.tensor_tensor(weight[:, :, :], first[:, :, :],
                                         rtotal[:, :].rearrange("p (a o) -> p a o", o=1).to_broadcast(every), ALU.mult))

            def products(g, tg, ft, started):
                dve.wait_ge(silu_done, FT * g + ft + 1)
                if started:
                    dve.wait_ge(g_lo_done, FT * (g - 1) + ft + 1)
                nc.vector.tensor_tensor(g_full[:, ft, :], silu[:, ft, :], h_ps[:, 1, ft, :], ALU.mult).then_inc(g_done, 1)

            def add(g, tg, e):
                for tt in range(GT):
                    dve.wait_ge(y_ready, GT * g + tt + 1)
                    i = GT * tg + tt
                    nc.vector.scalar_tensor_tensor(
                        out=tiles[:, i, :], in0=y_ps[:, tt, :],
                        scalar=weight[:, i, bass.ds(e, 1)], in1=tiles[:, i, :],
                        op0=ALU.mult, op1=ALU.add).then_inc(added, 1)

            def pair(i, is_first, is_last):
                for par in range(2):
                    e = 2 * i + par
                    for tg in range(GROUPS):
                        g = GROUPS * e + tg
                        started = not (is_first and par == 0 and tg == 0)
                        for ft in range(FT):
                            products(g, tg, ft, started)
                        if started:
                            add(g - 1, (tg - 1) % GROUPS, e if tg else e - 1)
                if is_last:
                    add(g, GROUPS - 1, e)

            over_pairs(dve, pair)

        @block.tensor
        def _(pe):
            pe.wait_ge(consts, 1)
            pe.wait_ge(wg_lo_ready, 1)
            with pe.Fori(0, GROUPS) as g:
                for tl in range(GT):
                    pe.wait_ge(xn_ready, GT * g + tl + 1)
                    for kt in range(KT):
                        last = nc.tensor.transpose(h_ps[:, 0, tl % 2, P * kt:P * (kt + 1)],
                                                   xn[tl % 2][:, P * kt:P * (kt + 1)], ident[:, :])
                    last.then_inc(xt_ready, 1)
                pe.wait_ge(lo_done, GT * (g + 1))
                cols = bass.ds(T * g, T)
                steps = [(w, xt, kt) for kt in range(KT)
                         for w, xt in ((wg_hi, xt_hi), (wg_hi, xt_lo), (wg_lo, xt_hi))]
                for n, (w, xt, kt) in enumerate(steps):
                    last = nc.tensor.matmul(y_ps[:, 0, :], w[:, kt, :],
                                            xt[:, kt:kt + 1, cols].rearrange("p o t -> p (o t)"),
                                            start=(n == 0), stop=(n == len(steps) - 1))
                last.then_inc(logits_ready, 1)
                pe.wait_ge(logits_done, g + 1)
                for tl in range(GT):
                    last = nc.tensor.transpose(y_ps[:, 1, P * tl:P * (tl + 1)], logits_t[:, P * tl:P * (tl + 1)],
                                               ident[:, :])
                last.then_inc(lt_ready, 1)

            def up(g, tg, e, par, started):
                if tg == 0:
                    pe.wait_ge(raw_split, e + 1)
                for ft in range(FT):
                    if started:
                        pe.wait_ge(g_done, FT * (g - 1) + ft + 1)
                    for which in range(2):
                        f0 = FF * which + P * ft
                        for kt in range(KT):
                            for w, xt in ((w13_hi, xt_hi), (w13_hi, xt_lo), (w13_lo, xt_hi)):
                                last = nc.tensor.matmul(h_ps[:, which, ft, :], w[par][:, kt, f0:f0 + P],
                                                        xt[:, kt, T * tg:T * (tg + 1)],
                                                        start=(kt == 0 and w is w13_hi and xt is xt_hi),
                                                        stop=(kt == KT - 1 and w is w13_lo))
                    last.then_inc(h_ready, 1)

            def down(g, tg, par, started):
                pe.wait_ge(g_lo_done, FT * (g + 1))
                for tt in range(GT):
                    if started:
                        pe.wait_ge(added, GT * (g - 1) + tt + 1)
                    cols = slice(P * tt, P * (tt + 1))
                    for ft in range(FT):
                        for gg, w in ((g_hi, w2_hi), (g_hi, w2_lo), (g_lo, w2_hi)):
                            last = nc.tensor.matmul(y_ps[:, tt, :], gg[tg % 2][:, ft, cols], w[par][:, ft, :],
                                                    start=(ft == 0 and gg is g_hi and w is w2_hi),
                                                    stop=(ft == FT - 1 and gg is g_lo))
                    last.then_inc(y_ready, 1)

            up(0, 0, 0, 0, False)

            def pair(i, is_first, is_last):
                for par in range(2):
                    e = 2 * i + par
                    for tg in range(GROUPS):
                        g = GROUPS * e + tg
                        if tg < GROUPS - 1:
                            up(g + 1, tg + 1, e, par, True)
                        elif not (is_last and par == 1):
                            up(g + 1, 0, e + 1, 1 - par, True)
                        down(g, tg, par, not (is_first and par == 0 and tg == 0))

            over_pairs(pe, pair)


def xattn_moe(nc, x, ctx_in, wq, bq, wk, bk, wv, bv, wo, bo, wg, w1, w3, w2, bias, out):
    q_scratch = nc.dram_tensor("q_scratch", [B, 2, PARTS, HD, H, T], BF16, kind="Internal").ap()
    o_scratch = nc.dram_tensor("o_scratch", [B, UNITS, P, T], F32, kind="Internal").ap()
    r_scratch = nc.dram_tensor("r_scratch", [B, H, T], F32, kind="Internal").ap()
    with nc.sbuf_tensor("x1", [P, B, CT, T], F32) as x1:
        attention(nc, x, ctx_in, wq, bq, wk, bk, wv, bv, wo, bo, x1, q_scratch, o_scratch, r_scratch)
        experts(nc, x1, wg, w1, w3, w2, bias, out)


def kernel(x, ctx_2048, L0_xattn_Wq, L0_xattn_bq, L0_xattn_Wk, L0_xattn_bk, L0_xattn_Wv, L0_xattn_bv,
           L0_xattn_Wo, L0_xattn_bo, L0_ffn_Wg, L0_ffn_W1, L0_ffn_W2, L0_ffn_W3, L0_ffn_bias):
    import numpy as np
    import concourse.bacc as bacc
    from concourse.bass_utils import run_bass_kernel_spmd

    def by_channel(w):
        w = np.asarray(w)
        return np.swapaxes(w.reshape(H, HD, *w.shape[1:]), 0, 1).reshape(w.shape)

    def column(v):
        return np.asarray(v).reshape(CT, P).T

    arrays = {
        "x": x, "ctx": ctx_2048,
        "wq": by_channel(L0_xattn_Wq).T, "bq": column(by_channel(L0_xattn_bq)),
        "wk": by_channel(L0_xattn_Wk).T, "bk": column(by_channel(L0_xattn_bk)),
        "wv": np.asarray(L0_xattn_Wv).T, "bv": column(L0_xattn_bv),
        "wo": np.asarray(L0_xattn_Wo).T, "bo": column(L0_xattn_bo),
        "wg": np.asarray(L0_ffn_Wg).T,
        "w1": np.swapaxes(np.asarray(L0_ffn_W1), 1, 2), "w3": np.swapaxes(np.asarray(L0_ffn_W3), 1, 2),
        "w2": np.swapaxes(np.asarray(L0_ffn_W2), 1, 2), "bias": np.asarray(L0_ffn_bias).reshape(1, E),
    }
    arrays = {f"in_{k}": np.ascontiguousarray(v) for k, v in arrays.items()}
    nc = bacc.Bacc("TRN2", target_bir_lowering=False, num_devices=1)
    args = [nc.dram_tensor(k, v.shape, mybir.dt.from_np(v.dtype), kind="ExternalInput").ap() for k, v in arrays.items()]
    out = nc.dram_tensor("out", [B, C, T], F32, kind="ExternalOutput").ap()
    xattn_moe(nc, *args, out)
    return run_bass_kernel_spmd(nc, [arrays], core_ids=[0]).results[0]["out"]
```

```python
import concourse.bass as bass
from concourse import mybir
from contextlib import ExitStack

F32 = mybir.dt.float32
F32R = mybir.dt.float32r
BF16 = mybir.dt.bfloat16
U32 = mybir.dt.uint32
ALU = mybir.AluOpType
ACT = mybir.ActivationFunctionType
AX = mybir.AxisListType

P = 128
B, C, T = 8, 256, 512
H, HD = 16, 16
CT = C // P
TT = T // P
UNITS, UH = 4, 4
SLOTS = UH * TT
PARTS = 3
QROWS = 6 * HD
KROWS = QROWS + PARTS
VW = 32
K_GROUPS = ((0, 3), (3, 2), (5, 1))
Q_GROUPS = ((0, 0, 3), (3, 1, 2), (5, 2, 1))
STACK_DMAS = len(K_GROUPS) + len(Q_GROUPS)
LAG = UNITS + 1
SCALE = 1.0 / HD ** 0.5
EPS = 1e-5
E, FF = 8, 256
KT = T // P
FT = FF // P
TOKENS = B * C
TILES = TOKENS // P
GT = 4
GROUPS = TILES // GT
TOP = 2
WG_COLS = 32
MIN_BLOCKS = 2
BLOCKS = TOP * TOKENS // P + MIN_BLOCKS * E
TABLE = BLOCKS + 1
SHIFT = P.bit_length() - 1


def attention(nc, x, ctx_in, wq, bq, wk, bk, wv, bv, wo, bo, x1, q_scratch, o_scratch, r_scratch):
    es = ExitStack()
    with es:
        def sb(name, shape, dt):
            return es.enter_context(nc.sbuf_tensor(name, shape, dt))

        def ps(name, shape):
            return es.enter_context(nc.psum_tensor(name, shape, F32))

        def sem(name):
            return es.enter_context(nc.semaphore(name))

        w_sb = {name: sb(f"{name}_sb", [P, CT, C], F32) for name in ("wq", "wk", "wv", "wo")}
        vecs = sb("vecs", [P, 4, CT], F32)
        bq_sb, bk_sb, bv_sb, bo_sb = (vecs[:, i, :] for i in range(4))
        bout = sb("bout", [P, CT], F32)
        ident = sb("ident", [P, P], F32)
        minus_half = sb("minus_half", [P, CT], F32)
        ctx_sb = sb("ctx_sb", [P, 2, CT, T], F32)
        xn = sb("xn", [P, CT, T], F32)
        stats = sb("stats", [P, CT, 6], F32)
        mean_var = sb("mean_var", [P, CT, 2], F32)
        var_eps = sb("var_eps", [P, CT], F32)
        pace = sb("pace", [P, 1], F32)
        rstd = sb("rstd", [P, CT], F32)
        qk = sb("qk", [P, 2, CT * T], F32)
        parts = sb("parts", [P, 2, PARTS, CT * T], BF16)
        qs = [sb(f"qs{i}", [P, H, T], BF16) for i in range(2)]
        ks = [sb(f"ks{i}", [P, H, T], BF16) for i in range(2)]
        v_sb = [sb(f"v{i}", [P, TT, H, VW], F32) for i in range(2)]
        neg_max = [sb(f"neg_max{i}", [P, H * TT], F32) for i in range(2)]
        m_rest = sb("m_rest", [H * TT, 2, P], F32)
        m_parts = sb("m_parts", [H * TT, PARTS, P], BF16)
        probs = sb("probs", [P, TT, UH, T], F32)
        o_sb = sb("o_sb", [P, 2, T], F32)
        den = sb("den", [P, 64], F32)
        rden = sb("rden", [P, 64], F32)
        o_heads = sb("o_heads", [P, CT, T], F32)
        r_heads = sb("r_heads", [P, CT, T], F32)
        o_norm = sb("o_norm", [P, CT, T], F32)

        st_ps = [ps(f"st_ps{i}", [P, 2, T]) for i in range(2)]
        s_ps = [ps(f"s_ps{i}", [P, T]) for i in range(2)]
        o_ps = ps("o_ps", [P, T])
        misc = ps("misc", [P, T])

        w_loaded = {name: sem(f"{name}_loaded") for name in ("wq", "wk", "wv", "wo")}
        vecs_loaded = sem("vecs_loaded")
        x_loaded = [sem(f"x_loaded{i}") for i in range(2)]
        ctx_loaded = [sem(f"ctx_loaded{i}") for i in range(2)]
        const_ready = sem("const_ready")
        ident_zero = sem("ident_zero")
        ident_ready = sem("ident_ready")
        stats_ready = sem("stats_ready")
        mv_ready = sem("mv_ready")
        eps_added = sem("eps_added")
        rstd_ready = sem("rstd_ready")
        xn_ready = sem("xn_ready")
        qk_ready, qk_done = sem("qk_ready"), sem("qk_done")
        part1, rest1, part2, part3 = sem("part1"), sem("rest1"), sem("part2"), sem("part3")
        parts_stored = [sem(f"parts_stored{i}") for i in range(2)]
        stack_loaded = [sem(f"stack_loaded{u}") for u in range(UNITS)]
        v_ready, v_done = sem("v_ready"), sem("v_done")
        s_ready, max_done = sem("s_ready"), sem("max_done")
        m_ready, m_part1, m_rest1, m_part2, m_rest2, m_done = (
            sem(n) for n in ("m_ready", "m_part1", "m_rest1", "m_part2", "m_rest2", "m_done"))
        m_loaded = sem("m_loaded")
        st_ready, exp_done = sem("st_ready"), sem("exp_done")
        pv_done, o_done = sem("pv_done"), sem("o_done")
        o_stored = [sem(f"o_stored{i}") for i in range(2)]
        den_loaded, rden_ready, rden_stored, heads_loaded = (
            sem(n) for n in ("den_loaded", "rden_ready", "rden_stored", "heads_loaded"))
        on_ready = sem("on_ready")
        wo_ready, wo_done = sem("wo_ready"), sem("wo_done")

        def x1_at(n, ct):
            v = x1[:, bass.ds(n, 1), ct, :]
            return v.rearrange("p o t -> p (o t)")

        def iterate(engine, step):
            for n in (0, 1):
                for u in range(UNITS):
                    step(n, n % 2, u, n // 2)
            with engine.Fori(1, 3) as i:
                for par in range(2):
                    for u in range(UNITS):
                        step(2 * i + par, par, u, i)
            for n in (6, 7, 8, 9):
                for u in range(UNITS):
                    step(n, n % 2, u, n // 2)

        def late(n, first):
            return n >= first if isinstance(n, int) else 2 >= first

        def early(n, last):
            return n <= last if isinstance(n, int) else 5 <= last

        def unit_runs(n, u):
            return not isinstance(n, int) or 0 <= UNITS * n + u - LAG < UNITS * B

        block = es.enter_context(nc.Block())


        @block.sync
        def _(sp):
            def load_x(m, par):
                sp.dma_start(x1[:, bass.ds(m, 1), :, :].rearrange("p o c t -> p (o c) t"),
                             x[bass.ds(m, 1)].rearrange("o (c p) t -> p (o c) t", p=P)).then_inc(x_loaded[par], 16)

            def load_ctx(m, par):
                sp.dma_start(ctx_sb[:, par, :, :],
                             ctx_in[bass.ds(m, 1)].rearrange("o (c p) t -> p (o c) t", p=P)).then_inc(ctx_loaded[par], 16)

            def store_parts(m, par):
                sp.wait_ge(part3, m + 1)
                sp.dma_start(q_scratch[bass.ds(m, 1)].rearrange("o w g (c k) h t -> (k h) (o w g c) t", c=CT),
                             parts[:, :, :, :].rearrange("p w g (c t) -> p (w g c) t", c=CT)
                             ).then_inc(parts_stored[par], 16)

            rows = q_scratch.rearrange("n w g k h t -> n w (g k) h t")

            def load_stack(m, par, i, u):
                if late(m, 2):
                    sp.wait_ge(pv_done, UNITS * TT * (m - 2) + TT * (u + 1))
                if u == 0:
                    sp.wait_ge(parts_stored[par], 16 * i + 16)
                heads = slice(UH * u, UH * (u + 1))

                for g, count in K_GROUPS:
                    src = rows[bass.ds(m, 1), 1, 0:HD * count, heads, :]
                    sp.dma_start(ks[par][HD * g:HD * (g + count), heads, :],
                                 src.rearrange("o r h t -> (o r) h t")).then_inc(stack_loaded[u], 16)
                for g, part, count in Q_GROUPS:
                    src = rows[bass.ds(m, 1), 0, HD * part:HD * (part + 1), heads, :]
                    sp.dma_start(qs[par][HD * g:HD * (g + count), heads, :],
                                 src.rearrange("o r h t -> o r (h t)").to_broadcast([count, HD, UH * T])
                                 ).then_inc(stack_loaded[u], 16)

            def load_m_rows(m, par):
                sp.wait_ge(m_done, m + 1)
                for g in range(PARTS):
                    sp.dma_start(qs[par][QROWS + g:QROWS + g + 1, :, :].rearrange("o h (a t) -> o (h a) t", a=TT),
                                 m_parts[:, g, :]).then_inc(m_loaded, 16)

            def store_o(n, u):
                tc = UNITS * n + u - LAG - 1
                m, mu = (n - 1, u - 2) if u >= 2 else (n - 2, u + 2)
                sp.wait_ge(o_done, tc + 1)
                sp.dma_start(o_scratch[bass.ds(m, 1), mu].rearrange("o r t -> (o r) t"),
                             o_sb[:, mu % 2, :]).then_inc(o_stored[mu % 2], 16)

            def load_den(m):
                for i in range(2):
                    sp.wait_ge(o_stored[i], 32 * (m + 1))
                den_rows = o_scratch.rearrange("n u (j r) t -> n (u j) r t", r=VW)
                sp.dma_start(den[:, :], den_rows[bass.ds(m, 1), :, HD, :].rearrange("o h t -> (o h) t")
                             ).then_inc(den_loaded, 16)
                for ct in range(CT):
                    src = den_rows[bass.ds(m, 1), 8 * ct:8 * (ct + 1), 0:HD, :]
                    sp.dma_start(o_heads[:, ct, :], src.rearrange("o h r t -> (o h) r t")).then_inc(heads_loaded, 16)
                sp.wait_ge(rden_ready, m + 1)
                sp.dma_start(r_scratch[bass.ds(m, 1)].rearrange("o h (a t) -> (o h a) t", a=8),
                             rden[:, :]).then_inc(rden_stored, 16)
                sp.wait_ge(rden_stored, 16 * (m + 1))
                for ct in range(CT):
                    src = r_scratch[bass.ds(m, 1), 8 * ct:8 * (ct + 1), :].rearrange("o (h r) t -> (o h) r t", r=1)
                    sp.dma_start(r_heads[:, ct, :], src.to_broadcast([8, HD, T])).then_inc(heads_loaded, 16)

            for name, src in (("wq", wq), ("wk", wk), ("wv", wv), ("wo", wo)):
                sp.dma_start(w_sb[name][:, :, :], src.rearrange("(c p) o -> p c o", p=P)).then_inc(w_loaded[name], 16)
                if name == "wq":
                    load_x(0, 0)
                    load_ctx(0, 0)
                    for vec, v in enumerate((bq, bk, bv, bo)):
                        sp.dma_start(vecs[:, vec, :], v.rearrange("p c -> p c")).then_inc(vecs_loaded, 16)
            load_x(1, 1)
            load_ctx(1, 1)
            store_parts(0, 0)
            load_stack(0, 0, 0, 0)
            load_stack(0, 0, 0, 1)

            def step(n, par, u, i):
                if unit_runs(n, u - 1) and u >= 0:
                    store_o(n, u)
                if u == 0 and early(n, 5):
                    load_x(n + 2, par)
                if u == 2 and early(n, 6):
                    load_stack(n + 1, 1 - par, i + par, 0)
                if u == 3 and early(n, 6):
                    load_stack(n + 1, 1 - par, i + par, 1)
                if u == 0 and early(n, 7):
                    load_stack(n, par, i, 2)
                if u == 1 and early(n, 7):
                    load_stack(n, par, i, 3)
                if u == 1 and late(n, 2):
                    load_den(n - 2)
                if u == 1 and early(n, 6):
                    store_parts(n + 1, 1 - par)
                if u == 0 and late(n, 1) and early(n, 8):
                    load_m_rows(n - 1, 1 - par)
                if u == 3 and early(n, 5):
                    sp.wait_ge(v_ready, 2 * (n + 1))
                    load_ctx(n + 2, par)

            iterate(sp, step)

        @block.gpsimd
        def _(pool):
            nc.gpsimd.memset(minus_half[:, :], -0.5)
            nc.gpsimd.memset(ident[:, :], 0.0).then_inc(ident_zero, 1)
            pool.wait_ge(ident_zero, 1)
            nc.gpsimd.affine_select(out=ident[:, :], in_=ident[:, :], compare_op=ALU.not_equal, fill=1.0, base=0,
                                    pattern=[[-1, P]], channel_multiplier=1).then_inc(ident_ready, 1)
            for buf in v_sb:
                nc.gpsimd.memset(buf[:, :, :, HD:VW], 1.0).then_inc(const_ready, 1)

            def norm_scale(m):
                pool.wait_ge(eps_added, m + 1)
                nc.gpsimd.tensor_tensor(rstd[:, :], var_eps[:, :], minus_half[:, :], ALU.pow).then_inc(rstd_ready, 1)

            def split(m):
                pool.wait_ge(part1, m + 1)
                nc.gpsimd.tensor_tensor(qk[:, :, :], qk[:, :, :], parts[:, :, 0, :], ALU.subtract).then_inc(rest1, 1)
                pool.wait_ge(part2, m + 1)
                nc.gpsimd.tensor_tensor(parts[:, :, 2, :], qk[:, :, :], parts[:, :, 1, :],
                                        ALU.subtract).then_inc(part3, 1)

            def normalize(m):
                pool.wait_ge(heads_loaded, 2 * CT * 16 * (m + 1))
                pool.wait_ge(wo_ready, CT * m + 1)
                nc.gpsimd.tensor_tensor(o_norm[:, :, :], o_heads[:, :, :], r_heads[:, :, :],
                                        ALU.mult).then_inc(on_ready, 1)

            norm_scale(0)
            norm_scale(1)
            split(0)

            def step(n, par, u, i):
                if u == 1 and early(n, 6):
                    split(n + 1)
                if u == 2 and late(n, 2):
                    normalize(n - 2)
                if u == 3 and early(n, 5):
                    norm_scale(n + 2)

            iterate(pool, step)

        @block.scalar
        def _(act):
            def evacuate_qk(m, j):
                act.wait_ge(qk_ready, 4 * m + j + 1)
                if j == 0 and late(m, 1):
                    act.wait_ge(part3, m)
                bias = (bq_sb, bk_sb)[j // CT][:, j % CT:j % CT + 1]
                nc.scalar.activation(qk[:, j // CT, T * (j % CT):T * (j % CT + 1)], misc[:, :], ACT.Identity,
                                     bias=bias).then_inc(qk_done, 1)

            def evacuate_v(m, par, j):
                act.wait_ge(v_ready, 2 * m + j + 1)
                if j == 0 and late(m, 2):
                    act.wait_ge(pv_done, UNITS * TT * (m - 1))
                nc.scalar.copy(v_sb[par][:, 2 * j:2 * j + 2, :, 0:HD],
                               misc[:, :].rearrange("p (s h k) -> p s h k", s=2, h=H)).then_inc(v_done, 1)

            def evacuate_o(tc, n, u):
                act.wait_ge(pv_done, TT * (tc + 1))
                if late(tc, 2):
                    act.wait_ge(o_stored[u % 2], 16 * (2 * n + (u - 6) // 2))
                nc.scalar.copy(o_sb[:, u % 2, :], o_ps[:, :]).then_inc(o_done, 1)

            act.wait_ge(vecs_loaded, 4 * 16)
            for j in range(2 * CT):
                evacuate_qk(0, j)

            def step(n, par, u, i):
                tc = UNITS * n + u - LAG
                for pair in range(SLOTS // 2):
                    if unit_runs(n, u):
                        g = (SLOTS // 2) * tc + pair
                        act.wait_ge(st_ready, g + 1)
                        if pair % 2 == 0 and late(tc, 1):
                            act.wait_ge(pv_done, TT * (tc - 1) + pair // 2 + 1)
                        half = 2 * (pair % 2)
                        nc.scalar.activation(probs[:, pair // 2, half:half + 2, :], st_ps[pair % 2][:, :, :], ACT.Exp,
                                             scale=SCALE).then_inc(exp_done, 1)
                    if pair == 2 and unit_runs(n, u - 1):
                        evacuate_o(tc - 1, n, u)
                    if early(n, 6) and u == 0 and pair in (2, 4, 6):
                        evacuate_qk(n + 1, pair // 2 - 1)
                    if early(n, 6) and u == 1 and pair == 2:
                        evacuate_qk(n + 1, 3)
                    if early(n, 7) and u == 2 and pair in (2, 5):
                        evacuate_v(n, par, pair // 4)

            iterate(act, step)

        @block.vector
        def _(dve):
            def norm_stats(m, par, i):
                dve.wait_ge(x_loaded[par], 16 * i + 16)
                for ct in range(CT):
                    nc.vector.bn_stats(stats[:, ct, :], x1_at(m, ct)).then_inc(stats_ready, 1)
                dve.wait_ge(stats_ready, CT * (m + 1))
                nc.vector.memset(pace[:, :], 0.0)
                for ct in range(CT):
                    nc.vector.bn_aggr(mean_var[:, ct, :], stats[:, ct, :]).then_inc(mv_ready, 1)
                dve.wait_ge(mv_ready, CT * (m + 1))
                nc.vector.tensor_scalar(var_eps[:, :], mean_var[:, :, 1], EPS, None, ALU.add).then_inc(eps_added, 1)

            def norm_apply(m):
                dve.wait_ge(rstd_ready, m + 1)
                if late(m, 1):
                    dve.wait_ge(qk_ready, 4 * (m - 1) + CT)
                for ct in range(CT):
                    nc.vector.tensor_scalar(xn[:, ct, :], x1_at(m, ct), mean_var[:, ct, 0:1], rstd[:, ct:ct + 1],
                                            ALU.subtract, ALU.mult).then_inc(xn_ready, 1)

            def round_first(m, par, i):
                dve.wait_ge(qk_done, 4 * (m + 1))
                if late(m, 1):
                    dve.wait_ge(parts_stored[1 - par], 16 * (i + par))
                nc.vector.tensor_copy(parts[:, :, 0, :], qk[:, :, :]).then_inc(part1, 1)

            def round_second(m):
                dve.wait_ge(rest1, m + 1)
                nc.vector.tensor_copy(parts[:, :, 1, :], qk[:, :, :]).then_inc(part2, 1)

            def split_max(m):
                dve.wait_ge(m_ready, m + 1)
                if late(m, 1):
                    dve.wait_ge(m_loaded, 16 * PARTS * m)
                mt = misc[0:H * TT, 0:P]
                nc.vector.tensor_copy(m_parts[:, 0, :], mt).then_inc(m_part1, 1)
                dve.wait_ge(m_part1, m + 1)
                nc.vector.tensor_tensor(m_rest[:, 0, :], mt, m_parts[:, 0, :], ALU.subtract).then_inc(m_rest1, 1)
                dve.wait_ge(m_rest1, m + 1)
                nc.vector.tensor_copy(m_parts[:, 1, :], m_rest[:, 0, :]).then_inc(m_part2, 1)
                dve.wait_ge(m_part2, m + 1)
                nc.vector.tensor_tensor(m_parts[:, 2, :], m_rest[:, 0, :], m_parts[:, 1, :],
                                        ALU.subtract).then_inc(m_done, 1)

            def add_residual(m, ot):
                dve.wait_ge(wo_ready, 1 + CT * m + ot + 1)
                nc.vector.scalar_tensor_tensor(out=x1_at(m, ot), in0=misc[:, :], scalar=bout[:, ot:ot + 1],
                                               in1=x1_at(m, ot), op0=ALU.add, op1=ALU.add).then_inc(wo_done, 1)

            for buf in ks:
                nc.vector.memset(buf[QROWS:KROWS, :, :], 1.0).then_inc(const_ready, 1)
            dve.wait_ge(vecs_loaded, 4 * 16)
            dve.wait_ge(wo_ready, 1)
            nc.vector.tensor_tensor(bout[:, :], misc[:, 0:CT], bo_sb, ALU.add).then_inc(wo_done, 1)
            norm_stats(0, 0, 0)
            norm_apply(0)
            norm_stats(1, 1, 0)
            norm_apply(1)
            round_first(0, 0, 0)
            round_second(0)

            def step(n, par, u, i):
                if early(n, 7) and u == 0 and late(n, 2):
                    dve.wait_ge(m_ready, n - 1)
                for slot in range(SLOTS):
                    if early(n, 7):
                        dve.wait_ge(s_ready, SLOTS * (UNITS * n + u) + slot + 1)
                        col = SLOTS * u + slot
                        nc.vector.tensor_reduce(neg_max[par][:, col:col + 1], s_ps[slot % 2][:, :], AX.X, ALU.max,
                                                negate=True).then_inc(max_done, 1)
                    if u == 0 and slot == 3 and late(n, 1) and early(n, 8):
                        split_max(n - 1)
                    if u == 1 and early(n, 6):
                        if slot == 7:
                            round_first(n + 1, 1 - par, i + par)
                        if slot == 13:
                            round_second(n + 1)
                    if u == 2 and slot == 0 and late(n, 2):
                        dve.wait_ge(den_loaded, 16 * (n - 1))
                        nc.vector.reciprocal(rden[:, :], den[:, :]).then_inc(rden_ready, 1)
                    if u == 3 and early(n, 5):
                        if slot == 1:
                            norm_stats(n + 2, par, i + 1)
                        if slot == 4:
                            norm_apply(n + 2)
                    if u == 3 and slot in (7, 13) and late(n, 2):
                        add_residual(n - 2, slot // 13)

            iterate(dve, step)

        @block.tensor
        def _(pe):
            def project_qk(m, par, i, j):
                which, ct_out = j // CT, j % CT
                w, src = (w_sb["wq"], xn) if which == 0 else (w_sb["wk"], ctx_sb[:, par])
                if j == 0:
                    pe.wait_ge(xn_ready, CT * (m + 1))
                    if late(m, 1):
                        pe.wait_ge(qk_done, 4 * m)
                    if late(m, 2):
                        pe.wait_ge(m_rest1, m - 1)
                if j == CT:
                    pe.wait_ge(ctx_loaded[par], 16 * i + 16)
                if j:
                    pe.wait_ge(qk_done, 4 * m + j)
                for ct in range(CT):
                    last = nc.tensor.matmul(misc[:, :], w[:, ct, P * ct_out:P * (ct_out + 1)], src[:, ct, :],
                                            start=(ct == 0), stop=(ct == CT - 1))
                last.then_inc(qk_ready, 1)

            def project_v(m, par, j):
                if j == 0:
                    if early(m, 6):
                        pe.wait_ge(qk_done, 4 * (m + 2))
                    else:
                        pe.wait_ge(m_rest1, m)
                else:
                    pe.wait_ge(v_done, 2 * m + 1)
                for half in range(2):
                    s0 = P * (2 * j + half)
                    for ct in range(CT):
                        last = nc.tensor.matmul(misc[:, C * half:C * (half + 1)], ctx_sb[:, par, ct, s0:s0 + P],
                                                w_sb["wv"][:, ct, :], start=(ct == 0), stop=(ct == CT - 1))
                last.then_inc(v_ready, 1)

            def project_out(m, ot):
                if ot == 0:
                    pe.wait_ge(on_ready, m + 1)
                    if early(m, 5):
                        pe.wait_ge(v_done, 2 * (m + 3))
                    else:
                        pe.wait_ge(m_rest1, B)
                pe.wait_ge(wo_done, 1 + CT * m + ot)
                for ct in range(CT):
                    last = nc.tensor.matmul(misc[:, :], w_sb["wo"][:, ct, P * ot:P * (ot + 1)], o_norm[:, ct, :],
                                            start=(ct == 0), stop=(ct == CT - 1))
                last.then_inc(wo_ready, 1)

            def wait_to_transpose(m):
                pe.wait_ge(max_done, UNITS * SLOTS * (m + 1))
                pe.wait_ge(v_done, 2 * (m + 1))
                if late(m, 2):
                    pe.wait_ge(wo_done, 1 + CT * (m - 1))

            def transpose_max(par):
                nc.tensor.transpose(misc[0:H * TT, 0:P], neg_max[par][:, :], ident[:, :]).then_inc(m_ready, 1)

            def weigh_values(tc, u, par, st):
                pe.wait_ge(exp_done, (SLOTS // 2) * tc + 2 * (st + 1))
                if st == 0 and late(tc, 1):
                    pe.wait_ge(o_done, tc)
                for j in range(UH):
                    last = nc.tensor.matmul(o_ps[VW * j:VW * (j + 1), :], v_sb[par][:, st, UH * u + j, :],
                                            probs[:, st, j, :], start=(st == 0), stop=(st == TT - 1),
                                            skip_group_check=True)
                last.then_inc(pv_done, 1)

            for name in ("wo", "wv"):
                pe.wait_ge(w_loaded[name], 16)
            pe.wait_ge(vecs_loaded, 4 * 16)
            for ot in range(CT):
                for ct in range(CT):
                    last = nc.tensor.matmul(misc[:, ot:ot + 1], w_sb["wo"][:, ct, P * ot:P * (ot + 1)],
                                            bv_sb[:, ct:ct + 1], start=(ct == 0), stop=(ct == CT - 1))
            last.then_inc(wo_ready, 1)
            for name in ("wq", "wk"):
                pe.wait_ge(w_loaded[name], 16)
            pe.wait_ge(ident_ready, 1)
            pe.wait_ge(const_ready, 4)
            pe.wait_ge(wo_done, 1)
            for j in range(2 * CT):
                project_qk(0, 0, 0, j)

            def step(n, par, u, i):
                tc = UNITS * n + u - LAG
                cu, cpar = (u - 1, 1 - par) if u else (UNITS - 1, par)
                if early(n, 7):
                    pe.wait_ge(stack_loaded[u], 16 * STACK_DMAS * (n + 1))
                if u == 1 and unit_runs(n, u):
                    pe.wait_ge(m_loaded, 16 * PARTS * n)
                    pe.wait_ge(v_done, 2 * n)
                for slot in range(SLOTS):
                    turns = u == 0 and slot == 2 and late(n, 1) and early(n, 8)
                    if turns:
                        wait_to_transpose(n - 1)
                    if early(n, 7):
                        g = SLOTS * (UNITS * n + u) + slot
                        if slot >= 2 or u >= 1 or late(n, 1):
                            pe.wait_ge(max_done, g - 1)
                        h, tt = UH * u + slot // TT, slot % TT
                        nc.tensor.matmul(s_ps[slot % 2][:, :], qs[par][0:QROWS, h, P * tt:P * (tt + 1)],
                                         ks[par][0:QROWS, h, :], start=True, stop=True).then_inc(s_ready, 1)
                    if unit_runs(n, u):
                        pair, half = slot // 2, slot % 2
                        if half == 0 and (pair >= 2 or late(tc, 1)):
                            pe.wait_ge(exp_done, (SLOTS // 2) * tc + pair - 1)
                        st, h = slot // UH, UH * cu + slot % UH
                        last = nc.tensor.matmul(st_ps[pair % 2][:, half, :], ks[cpar][0:KROWS, h, P * st:P * (st + 1)],
                                                qs[cpar][0:KROWS, h, :], start=True, stop=True)
                        if half == 1:
                            last.then_inc(st_ready, 1)
                    if slot == 3 and unit_runs(n, u - 1):
                        pu, ppar = (cu - 1, cpar) if cu else (UNITS - 1, 1 - cpar)
                        weigh_values(tc - 1, pu, ppar, TT - 1)
                    if slot % UH == UH - 1 and slot > UH and unit_runs(n, u):
                        weigh_values(tc, cu, cpar, slot // UH - 1)
                    if turns:
                        transpose_max(1 - par)
                    if early(n, 6) and u == 0 and slot in (4, 8, 12):
                        project_qk(n + 1, 1 - par, i + par, slot // 4 - 1)
                    if early(n, 6) and u == 1 and slot == 4:
                        project_qk(n + 1, 1 - par, i + par, 3)
                    if early(n, 7) and u == 2 and slot in (4, 10):
                        project_v(n, par, slot // 10)
                    if late(n, 2) and u == 3 and slot in (6, 12):
                        project_out(n - 2, slot // 12)

            iterate(pe, step)


def experts(nc, x1, xn_rows, wg, w1, w3, w2, bias, out):
    es = ExitStack()
    with es:
        def sb(name, shape, dt):
            return es.enter_context(nc.sbuf_tensor(name, shape, dt))

        def ps(name, shape):
            return es.enter_context(nc.psum_tensor(name, shape, F32))

        def sem(name):
            return es.enter_context(nc.semaphore(name))

        w13_raw = sb("w13_raw", [P, KT, 2 * FF], F32)
        w2_raw = sb("w2_raw", [P, FT, T], F32)
        w13_hi = [sb(f"w13_hi{i}", [P, KT, 2 * FF], F32R) for i in range(2)]
        w13_lo = [sb(f"w13_lo{i}", [P, KT, 2 * FF], F32R) for i in range(2)]
        w2_hi = [sb(f"w2_hi{i}", [P, FT, T], F32R) for i in range(2)]
        w2_lo = [sb(f"w2_lo{i}", [P, FT, T], F32R) for i in range(2)]
        ident = sb("ident2", [P, P], F32)
        minus_half = sb("minus_half2", [P, GT], F32)
        stats = sb("stats2", [P, GT, 6], F32)
        mean_var = sb("mean_var2", [P, GT, 2], F32)
        var_eps = sb("var_eps2", [P, GT], F32)
        pace = sb("pace2", [P, 1], F32)
        pause = sb("pause", [P, 3], F32)
        rstd = sb("rstd2", [P, GT], F32)
        xn = sb("xn2", [P, GT, T], F32)
        xt = sb("xt", [P, KT, GT, P], F32)
        wg_sb = sb("wg_sb", [P, KT, WG_COLS], F32)
        logits_t = sb("logits_t", [P, T], F32)
        logits = sb("logits", [P, TILES, E], F32)
        bias_row = sb("bias_row", [P, E], F32)
        lanes = sb("lanes", [P, P], F32)
        token_1 = sb("token_1", [P, TILES], F32)
        below = sb("below", [P, P], BF16)
        ones = sb("ones", [P, P], BF16)
        route = sb("route", [P, TILES, E], F32)
        score = sb("score", [P, TILES, E], F32)
        top = sb("top", [P, TILES, E], F32)
        top_at = sb("top_at", [P, TILES, E], U32)
        top_lane = sb("top_lane", [P, TOP, TILES], F32)
        chosen = sb("chosen", [P, TOP, TILES, E], F32)
        mask = sb("mask", [P, TILES, E], BF16)
        picked = sb("picked", [P, TOP, TILES, E], F32)
        top_route = sb("top_route", [P, TOP, TILES], F32)
        total = sb("total", [P, TILES], F32)
        rtotal = sb("rtotal", [P, TILES], F32)
        weight = sb("weight", [P, TOP, TILES], F32)
        before = sb("before", [P, TILES + 1, E], F32)
        rounded = sb("rounded", [P, E], U32)
        blocks_i = sb("blocks_i", [P, E], U32)
        blocks_f = sb("blocks_f", [P, E], F32)
        start = sb("start", [P, E + 1], F32)
        spans = sb("spans", [P, 2 * E + 1], mybir.dt.int32)
        place = sb("place", [P, TILES, E], F32)
        slot_f = sb("slot_f", [P, TOP * TILES], F32)
        slot_i = sb("slot_i", [P, TOP * TILES], U32)
        row_i = sb("row_i", [P, TOP * TILES], U32)
        block_i = sb("block_i", [P, TOP * TILES], U32)
        row_f = sb("row_f", [P, TOP * TILES], F32)
        block_f = sb("block_f", [P, TOP * TILES], F32)
        row_hot = sb("row_hot", [P, TOP * TILES, P], F32)
        block_hot = sb("block_hot", [P, TOP * TILES, BLOCKS], F32)
        entries = sb("entries", [P, TOP * TILES, 2, BLOCKS], F32)
        empty = sb("empty", [P, BLOCKS], F32)
        id_1 = sb("id_1", [P, BLOCKS], F32)
        ids = sb("ids", [P, 2 * TABLE], U32)
        block_weight = sb("block_weight", [P, 2 * TABLE], F32)
        id_in = sb("id_in", [P, 1], U32)
        id_out = sb("id_out", [P, 1], U32)
        rows = sb("rows", [P, T], F32)
        xb_hi = sb("xb_hi", [P, KT, P], F32R)
        xb_lo = sb("xb_lo", [P, KT, P], F32R)
        silu = sb("silu", [P, FF], F32)
        g = sb("g", [P, FF], F32)
        gt_hi = sb("gt_hi", [P, FT, P], F32R)
        gt_lo = sb("gt_lo", [P, FT, P], F32R)
        y_sb = sb("y_sb", [P, T], F32)

        t_ps = ps("t_ps", [P, 2, T])
        h_ps = ps("h_ps", [P, T])
        y_ps = ps("y_ps", [P, T])
        gt_ps = ps("gt_ps", [P, FT, P])
        logits_ps = ps("logits_ps", [P, T])
        lt_ps = ps("lt_ps", [P, GT, KT, WG_COLS])
        rank_ps = ps("rank_ps", [P, T])

        route_loaded, raw_loaded = sem("route_loaded"), sem("raw_loaded")
        wg_zero, ident_zero, consts, below_ones = sem("wg_zero"), sem("ident_zero2"), sem("consts"), sem("below_ones")
        rows_zero, ids_empty = sem("rows_zero"), sem("ids_empty")
        stats_ready, mv_ready, eps_added, rstd_ready = (
            sem(n) for n in ("stats_ready2", "mv_ready2", "eps_added2", "rstd_ready2"))
        xn_ready, xn_stored, xt_ready, xt_done = sem("xn_ready2"), sem("xn_stored"), sem("xt_ready"), sem("xt_done")
        logits_ready, logits_done, lt_ready, lt_done = (
            sem(n) for n in ("logits_ready", "logits_done", "lt_ready", "lt_done"))
        routed, chain, mask_ready, rank_ready = sem("routed"), sem("chain"), sem("mask_ready"), sem("rank_ready")
        spans_ready, entries_ready, table_summed, table_ready = (
            sem(n) for n in ("spans_ready", "entries_ready", "table_summed", "table_ready"))
        w13_hi_cut, w13_cut, w2_hi_cut, w2_cut = (sem(n) for n in ("w13_hi_cut", "w13_cut", "w2_hi_cut", "w2_cut"))
        id_in_ready, id_out_ready, gathered = sem("id_in_ready"), sem("id_out_ready"), sem("gathered")
        t_ready, xb_hi_done, xb_done = sem("t_ready"), sem("xb_hi_done"), sem("xb_done")
        h_ready, silu_done, g_done = sem("h_ready"), sem("silu_done"), sem("g_done")
        gt_ready, gt_hi_done, gt_done = sem("gt_ready"), sem("gt_hi_done"), sem("gt_done")
        y_ready, y_done = sem("y_ready"), sem("y_done")
        out_written = sem("out_written")

        tiles = x1[:, :, :, :].rearrange("p n c t -> p (n c) t")
        out_rows = out.rearrange("n c t -> (n c) t")
        in_rows = xn_rows.rearrange("n c t -> (n c) t")

        def f32(ap):
            return ap.bitcast(F32)

        def tile_at(i):
            return tiles[:, bass.ds(i, 1), :].rearrange("p o t -> p (o t)")

        def load_span(engine, e):
            count = engine.value_load(spans[0:1, bass.ds(e, 1)], min_val=MIN_BLOCKS, max_val=BLOCKS)
            first = engine.value_load(spans[0:1, bass.ds(E + e, 1)], min_val=0, max_val=BLOCKS)
            return count, first

        def load_tail(engine):
            return engine.value_load(spans[0:1, 2 * E:2 * E + 1], min_val=MIN_BLOCKS * E - 2, max_val=BLOCKS - 2)

        def over_blocks(engine, block):
            def expert(e, par, started, has_next):
                count, first = load_span(engine, e)
                block(first if started else 0, e, par, True, started, has_next)
                with engine.Fori(1, count) as j:
                    block(first + j, e, par, False, True, has_next)

            expert(0, 0, False, True)
            expert(1, 1, True, True)
            with engine.Fori(1, E // 2 - 1) as i:
                expert(2 * i, 0, True, True)
                expert(2 * i + 1, 1, True, True)
            expert(E - 2, 0, True, True)
            expert(E - 1, 1, True, False)

        block = es.enter_context(nc.Block())

        @block.sync
        def _(sp):
            sp.wait_ge(wg_zero, 1)
            sp.dma_start(wg_sb[:, :, 0:E], wg.rearrange("(k p) e -> p k e", p=P)).then_inc(route_loaded, 16)
            sp.dma_start(bias_row[:, :], bias.to_broadcast([P, E])).then_inc(route_loaded, 16)

            def load(e):
                sp.dma_start(w13_raw[:, :, 0:FF], w1[bass.ds(e, 1)].rearrange("o (k p) f -> p (o k) f", p=P)
                             ).then_inc(raw_loaded, 16)
                sp.dma_start(w13_raw[:, :, FF:2 * FF], w3[bass.ds(e, 1)].rearrange("o (k p) f -> p (o k) f", p=P)
                             ).then_inc(raw_loaded, 16)
                sp.dma_start(w2_raw[:, :, :], w2[bass.ds(e, 1)].rearrange("o (k p) t -> p (o k) t", p=P)
                             ).then_inc(raw_loaded, 16)

            load(0)
            with sp.Fori(0, GROUPS) as gr:
                sp.wait_ge(xn_ready, GT * (gr + 1))
                sp.dma_start(xn_rows[bass.ds(gr * (GT // CT), GT // CT)].rearrange("n (c p) t -> p (n c) t", p=P),
                             xn[:, :, :]).then_inc(xn_stored, 16)
            with sp.Fori(1, E) as e:
                sp.wait_ge(w13_cut, e)
                sp.wait_ge(w2_cut, e)
                load(e)

        @block.gpsimd
        def _(pool):
            nc.gpsimd.dma_start(out.rearrange("n (c p) t -> p (n c) t", p=P), tiles).then_inc(out_written, 16)
            nc.gpsimd.memset(minus_half[:, :], -0.5)
            nc.gpsimd.memset(ones[:, :], 1.0)
            nc.gpsimd.memset(below[:, :], 1.0).then_inc(below_ones, 1)
            nc.gpsimd.memset(ident[:, :], 0.0).then_inc(ident_zero, 1)
            pool.wait_ge(ident_zero, 1)
            nc.gpsimd.affine_select(out=ident[:, :], in_=ident[:, :], compare_op=ALU.not_equal, fill=1.0, base=0,
                                    pattern=[[-1, P]], channel_multiplier=1).then_inc(consts, 1)
            pool.wait_ge(below_ones, 1)
            nc.gpsimd.affine_select(out=below[:, :], in_=below[:, :], compare_op=ALU.is_gt, fill=0.0, base=0,
                                    pattern=[[1, P]], channel_multiplier=-1).then_inc(consts, 1)
            nc.gpsimd.iota(lanes[:, :], pattern=[[1, P]], base=0, channel_multiplier=0,
                           allow_small_or_imprecise_dtypes=True).then_inc(consts, 1)
            nc.gpsimd.iota(token_1[:, :], pattern=[[P, TILES]], base=1, channel_multiplier=1,
                           allow_small_or_imprecise_dtypes=True).then_inc(consts, 1)
            nc.gpsimd.memset(rows[:, :], 0.0).then_inc(rows_zero, 1)
            nc.gpsimd.memset(ids[:, BLOCKS:TABLE], 2 * TOKENS - 1).then_inc(ids_empty, 1)
            with pool.Fori(0, GROUPS) as gr:
                pool.wait_ge(eps_added, gr + 1)
                nc.gpsimd.tensor_tensor(rstd[:, :], var_eps[:, :], minus_half[:, :], ALU.pow).then_inc(rstd_ready, 1)

            def gather(b):
                nc.gpsimd.tensor_copy(id_in[:, :], ids[:, bass.ds(b, 1)]).then_inc(id_in_ready, 1)
                pool.wait_ge(id_in_ready, b + 1)
                nc.gpsimd.tensor_tensor(pause[:, 0:1], minus_half[:, 0:1], minus_half[:, 0:1], ALU.add)
                pool.wait_ge(xn_stored, 16 * GROUPS)
                nc.gpsimd.indirect_dma_start(rows[:, :], None, in_rows,
                                             bass.IndirectOffsetOnAxis(ap=id_in[:, 0:1], axis=0),
                                             bounds_check=TOKENS - 1, oob_is_err=False).then_inc(gathered, 16)

            def scatter(b):
                pool.wait_ge(out_written, 16 * (b + 1))
                nc.gpsimd.tensor_copy(id_out[:, :], ids[:, bass.ds(b, 1)]).then_inc(id_out_ready, 1)
                pool.wait_ge(y_done, b + 1)
                pool.wait_ge(id_out_ready, b + 1)
                nc.gpsimd.tensor_tensor(pause[:, 1:2], minus_half[:, 0:1], minus_half[:, 0:1], ALU.add)
                nc.gpsimd.indirect_dma_start(out_rows, bass.IndirectOffsetOnAxis(ap=id_out[:, 0:1], axis=0),
                                             y_sb[:, :], None, bounds_check=TOKENS - 1, oob_is_err=False,
                                             compute_op=ALU.add).then_inc(out_written, 16)

            pool.wait_ge(spans_ready, 3)
            pool.wait_ge(table_ready, 1)
            pool.wait_ge(rows_zero, 1)
            tail = load_tail(pool)
            gather(0)
            for b in (0, 1):
                pool.wait_ge(t_ready, b + 1)
                gather(b + 1)
            with pool.Fori(0, tail) as b:
                pool.wait_ge(t_ready, b + 3)
                gather(b + 3)
                scatter(b)
            scatter(tail)
            scatter(tail + 1)
            pool.wait_ge(out_written, 16 * (tail + 3))
            nc.gpsimd.tensor_tensor(pause[:, 2:3], minus_half[:, 0:1], minus_half[:, 0:1], ALU.add)

        @block.scalar
        def _(act):
            def cut_w13(e, par):
                act.wait_ge(raw_loaded, 48 * (e + 1))
                nc.scalar.copy(w13_hi[par][:, :, :], w13_raw[:, :, :]).then_inc(w13_hi_cut, 1)

            def cut_w2(e, par):
                nc.scalar.copy(w2_hi[par][:, :, :], w2_raw[:, :, :]).then_inc(w2_hi_cut, 1)

            cut_w13(0, 0)
            cut_w2(0, 0)

            def group(gr, is_first):
                for tl in range(GT):
                    act.wait_ge(xt_ready, GT * gr + tl + 1)
                    if tl == 0 and not is_first:
                        act.wait_ge(logits_ready, gr)
                    nc.scalar.copy(xt[:, :, tl, :], t_ps[:, tl % 2, :].rearrange("p (k t) -> p k t", k=KT)
                                   ).then_inc(xt_done, 1)
                act.wait_ge(logits_ready, gr + 1)
                nc.scalar.copy(logits_t[:, :], logits_ps[:, :]).then_inc(logits_done, 1)

            group(0, True)
            with act.Fori(1, GROUPS) as gr:
                group(gr, False)
            act.wait_ge(lt_done, GROUPS)
            nc.scalar.activation(route[:, :, :], logits[:, :, :], ACT.Sigmoid).then_inc(routed, 1)
            act.wait_ge(spans_ready, 3)

            def split_rows(b):
                act.wait_ge(t_ready, b + 1)
                nc.scalar.copy(xb_hi[:, :, :], t_ps[:, 0, :].rearrange("p (k t) -> p k t", k=KT)
                               ).then_inc(xb_hi_done, 1)

            def take_y(b):
                act.wait_ge(out_written, 16 * (b + 1))
                act.wait_ge(y_ready, b + 1)
                nc.scalar.copy(y_sb[:, :], y_ps[:, :]).then_inc(y_done, 1)

            def step(b, e, par, opens, started, has_next):
                act.wait_ge(h_ready, b + 1)
                nc.scalar.activation(silu[:, :], h_ps[:, 0:FF], ACT.Silu).then_inc(silu_done, 1)
                split_rows(b + 1)
                if opens and has_next:
                    cut_w13(e + 1, 1 - par)
                if started:
                    take_y(b - 1)
                act.wait_ge(gt_ready, b + 1)
                nc.scalar.copy(gt_hi[:, :, :], gt_ps[:, :, :]).then_inc(gt_hi_done, 1)
                if opens and has_next:
                    cut_w2(e + 1, 1 - par)

            split_rows(0)
            over_blocks(act, step)
            take_y(load_tail(act) + 1)

        @block.vector
        def _(dve):
            def cut_w13(e, par):
                dve.wait_ge(w13_hi_cut, e + 1)
                nc.vector.tensor_tensor(w13_lo[par][:, :, :], w13_raw[:, :, :], f32(w13_hi[par][:, :, :]),
                                        ALU.subtract).then_inc(w13_cut, 1)

            def cut_w2(e, par):
                dve.wait_ge(w2_hi_cut, e + 1)
                nc.vector.tensor_tensor(w2_lo[par][:, :, :], w2_raw[:, :, :], f32(w2_hi[par][:, :, :]),
                                        ALU.subtract).then_inc(w2_cut, 1)

            nc.vector.memset(wg_sb[:, :, :], 0.0).then_inc(wg_zero, 1)

            def take_logits(gr):
                dve.wait_ge(lt_ready, gr + 1)
                nc.vector.tensor_reduce(logits[:, bass.ds(GT * gr, GT), :],
                                        lt_ps[:, :, :, 0:E].rearrange("p a k e -> p a e k"),
                                        AX.X, ALU.add).then_inc(lt_done, 1)

            def group(gr, is_first):
                for tl in range(GT):
                    nc.vector.bn_stats(stats[:, tl, :], tile_at(GT * gr + tl)).then_inc(stats_ready, 1)
                dve.wait_ge(stats_ready, GT * gr + GT)
                nc.vector.memset(pace[:, :], 0.0)
                for tl in range(GT):
                    nc.vector.bn_aggr(mean_var[:, tl, :], stats[:, tl, :]).then_inc(mv_ready, 1)
                dve.wait_ge(mv_ready, GT * gr + GT)
                nc.vector.tensor_scalar(var_eps[:, :], mean_var[:, :, 1], EPS, None, ALU.add).then_inc(eps_added, 1)
                dve.wait_ge(rstd_ready, gr + 1)
                for tl in range(GT):
                    if tl == 0 and not is_first:
                        dve.wait_ge(xn_stored, 16 * gr)
                        dve.wait_ge(xt_ready, GT * gr)
                    nc.vector.tensor_scalar(xn[:, tl, :], tile_at(GT * gr + tl), mean_var[:, tl, 0:1],
                                            rstd[:, tl:tl + 1], ALU.subtract, ALU.mult).then_inc(xn_ready, 1)
                if not is_first:
                    take_logits(gr - 1)

            group(0, True)
            cut_w13(0, 0)
            cut_w2(0, 0)
            with dve.Fori(1, GROUPS) as gr:
                group(gr, False)
            take_logits(GROUPS - 1)
            count = [0]

            def link(instruction):
                count[0] += 1
                instruction.then_inc(chain, 1)
                dve.wait_ge(chain, count[0])

            def spread(ap, shape):
                return ap.to_broadcast(shape)

            every = [P, TILES, E]
            both = [P, TOP, TILES, E]
            dve.wait_ge(routed, 1)
            dve.wait_ge(route_loaded, 32)
            dve.wait_ge(consts, 4)
            link(nc.vector.tensor_tensor(score[:, :, :], route[:, :, :],
                                         spread(bias_row[:, :].rearrange("p (o e) -> p o e", o=1), every), ALU.add))
            for i in range(TILES):
                last = nc.vector.max(top[:, i, :], score[:, i, :])
            link(last)
            for i in range(TILES):
                last = nc.vector.max_index(top_at[:, i, :], top[:, i, :], score[:, i, :])
            link(last)
            link(nc.vector.tensor_copy(top_lane[:, :, :], top_at[:, :, 0:TOP].rearrange("p i k -> p k i")))
            link(nc.vector.tensor_tensor(
                chosen[:, :, :, :].rearrange("p k i e -> p (k i) e"),
                spread(lanes[:, 0:E].rearrange("p (o e) -> p o e", o=1), [P, TOP * TILES, E]),
                spread(top_lane[:, :, :].rearrange("p k (i o) -> p (k i) o", o=1), [P, TOP * TILES, E]), ALU.is_equal))
            link(nc.vector.tensor_tensor(mask[:, :, :], chosen[:, 0, :, :], chosen[:, 1, :, :], ALU.add))
            nc.vector.memset(pace[:, :], 0.0).then_inc(mask_ready, 1)
            for k in range(TOP):
                nc.vector.tensor_tensor(picked[:, k, :, :], chosen[:, k, :, :], route[:, :, :],
                                        ALU.mult).then_inc(chain, 1)
            count[0] += TOP
            dve.wait_ge(chain, count[0])
            link(nc.vector.tensor_reduce(top_route[:, :, :].rearrange("p k i -> p (k i)"),
                                         picked[:, :, :, :].rearrange("p k i e -> p (k i) e"), AX.X, ALU.add))
            link(nc.vector.tensor_tensor(total[:, :], top_route[:, 0, :], top_route[:, 1, :], ALU.add))
            link(nc.vector.reciprocal(rtotal[:, :], total[:, :]))
            link(nc.vector.tensor_tensor(weight[:, :, :], top_route[:, :, :],
                                         spread(rtotal[:, :].rearrange("p (o i) -> p o i", o=1), [P, TOP, TILES]),
                                         ALU.mult))
            link(nc.vector.memset(before[:, 0, :], 0.0))
            dve.wait_ge(rank_ready, 1)
            in_tile = rank_ps[:, P:2 * P].rearrange("p (i e) -> p i e", e=E)
            for i in range(TILES):
                link(nc.vector.tensor_tensor(before[:, i + 1, :], before[:, i, :], in_tile[:, i, :], ALU.add))
            link(nc.vector.tensor_scalar(rounded[:, :], before[:, TILES, :], float(P - 1), None, ALU.add))
            link(nc.vector.tensor_scalar(blocks_i[:, :], rounded[:, :], SHIFT, None, ALU.logical_shift_right))
            link(nc.vector.tensor_scalar(blocks_f[:, :], blocks_i[:, :], float(MIN_BLOCKS), None, ALU.max))
            link(nc.vector.memset(start[:, 0:1], 0.0))
            for e in range(E):
                link(nc.vector.tensor_tensor(start[:, e + 1:e + 2], start[:, e:e + 1], blocks_f[:, e:e + 1], ALU.add))
            nc.vector.tensor_copy(spans[:, 0:E], blocks_f[:, :]).then_inc(spans_ready, 1)
            nc.vector.tensor_copy(spans[:, E:2 * E], start[:, 0:E]).then_inc(spans_ready, 1)
            nc.vector.tensor_scalar(spans[:, 2 * E:2 * E + 1], start[:, E:E + 1], -2.0, None,
                                    ALU.add).then_inc(spans_ready, 1)
            link(nc.vector.tensor_tensor(place[:, :, :], rank_ps[:, 0:P].rearrange("p (i e) -> p i e", e=E),
                                         before[:, 0:TILES, :], ALU.add))
            link(nc.vector.scalar_tensor_tensor(
                out=place[:, :, :], in0=spread(start[:, 0:E].rearrange("p (o e) -> p o e", o=1), every),
                scalar=float(P), in1=place[:, :, :], op0=ALU.mult, op1=ALU.add))
            for k in range(TOP):
                nc.vector.tensor_tensor(picked[:, k, :, :], chosen[:, k, :, :], place[:, :, :],
                                        ALU.mult).then_inc(chain, 1)
            count[0] += TOP
            dve.wait_ge(chain, count[0])
            link(nc.vector.tensor_reduce(slot_f[:, :], picked[:, :, :, :].rearrange("p k i e -> p (k i) e"),
                                         AX.X, ALU.add))
            link(nc.vector.tensor_copy(slot_i[:, :], slot_f[:, :]))
            link(nc.vector.tensor_scalar(block_i[:, :], slot_i[:, :], SHIFT, None, ALU.logical_shift_right))
            link(nc.vector.tensor_scalar(row_i[:, :], slot_i[:, :], P - 1, None, ALU.bitwise_and))
            link(nc.vector.tensor_copy(block_f[:, :], block_i[:, :]))
            link(nc.vector.tensor_copy(row_f[:, :], row_i[:, :]))
            hot = [P, TOP * TILES, BLOCKS]
            link(nc.vector.tensor_tensor(block_hot[:, :, :], spread(lanes[:, 0:BLOCKS].rearrange("p (o b) -> p o b", o=1), hot),
                                         spread(block_f[:, :].rearrange("p (j o) -> p j o", o=1), hot), ALU.is_equal))
            for k in range(TOP):
                js = slice(TILES * k, TILES * (k + 1))
                nc.vector.tensor_tensor(entries[:, js, 0, :], block_hot[:, js, :],
                                        spread(token_1[:, :].rearrange("p (i o) -> p i o", o=1), [P, TILES, BLOCKS]),
                                        ALU.mult).then_inc(entries_ready, 1)
            nc.vector.tensor_tensor(entries[:, :, 1, :], block_hot[:, :, :],
                                    spread(weight[:, :, :].rearrange("p k (i o) -> p (k i) o", o=1), hot),
                                    ALU.mult).then_inc(entries_ready, 1)
            hot = [P, TOP * TILES, P]
            nc.vector.tensor_tensor(row_hot[:, :, :], spread(lanes[:, :].rearrange("p (o b) -> p o b", o=1), hot),
                                    spread(row_f[:, :].rearrange("p (j o) -> p j o", o=1), hot),
                                    ALU.is_equal).then_inc(entries_ready, 1)
            dve.wait_ge(table_summed, 1)
            link(nc.vector.tensor_scalar(empty[:, :], rank_ps[:, 2 * P:2 * P + BLOCKS], 0.0, float(2 * TOKENS),
                                         ALU.is_equal, ALU.mult))
            link(nc.vector.tensor_tensor(id_1[:, :], empty[:, :], rank_ps[:, 2 * P:2 * P + BLOCKS], ALU.add))
            link(nc.vector.tensor_copy(block_weight[:, 0:BLOCKS], rank_ps[:, 2 * P + BLOCKS:2 * P + 2 * BLOCKS]))
            nc.vector.tensor_scalar(ids[:, 0:BLOCKS], id_1[:, :], -1.0, None, ALU.add).then_inc(table_ready, 1)

            dve.wait_ge(spans_ready, 3)

            def split_rows(b):
                dve.wait_ge(xb_hi_done, b + 1)
                nc.vector.tensor_tensor(xb_lo[:, :, :], t_ps[:, 0, :].rearrange("p (k t) -> p k t", k=KT),
                                        f32(xb_hi[:, :, :]), ALU.subtract).then_inc(xb_done, 1)

            def step(b, e, par, opens, started, has_next):
                dve.wait_ge(silu_done, b + 1)
                nc.vector.scalar_tensor_tensor(out=g[:, :], in0=silu[:, :], scalar=block_weight[:, bass.ds(b, 1)],
                                               in1=h_ps[:, FF:2 * FF], op0=ALU.mult, op1=ALU.mult).then_inc(g_done, 1)
                split_rows(b + 1)
                if opens and has_next:
                    cut_w13(e + 1, 1 - par)
                dve.wait_ge(gt_hi_done, b + 1)
                nc.vector.tensor_tensor(gt_lo[:, :, :], gt_ps[:, :, :], f32(gt_hi[:, :, :]),
                                        ALU.subtract).then_inc(gt_done, 1)
                if opens and has_next:
                    cut_w2(e + 1, 1 - par)

            split_rows(0)
            over_blocks(dve, step)

        @block.tensor
        def _(pe):
            def group(gr, is_first):
                for tl in range(GT):
                    pe.wait_ge(xn_ready, GT * gr + tl + 1)
                    if tl >= 2 or not is_first:
                        pe.wait_ge(xt_done, GT * gr + tl - 1)
                    for kt in range(KT):
                        last = nc.tensor.transpose(t_ps[:, tl % 2, P * kt:P * (kt + 1)],
                                                   xn[:, tl, P * kt:P * (kt + 1)], ident[:, :])
                    last.then_inc(xt_ready, 1)
                pe.wait_ge(xt_done, GT * (gr + 1))
                if not is_first:
                    pe.wait_ge(logits_done, gr)
                for kt in range(KT):
                    last = nc.tensor.matmul(logits_ps[WG_COLS * kt:WG_COLS * (kt + 1), :], wg_sb[:, kt, :],
                                            xt[:, kt, :, :].rearrange("p a t -> p (a t)"),
                                            start=True, stop=True, skip_group_check=True)
                last.then_inc(logits_ready, 1)
                pe.wait_ge(logits_done, gr + 1)
                if not is_first:
                    pe.wait_ge(lt_done, gr)
                for tl in range(GT):
                    last = nc.tensor.transpose(lt_ps[:, tl, :, :].rearrange("p k e -> p (k e)"),
                                               logits_t[:, P * tl:P * (tl + 1)], ident[:, :])
                last.then_inc(lt_ready, 1)

            pe.wait_ge(consts, 2)
            pe.wait_ge(route_loaded, 32)
            group(0, True)
            with pe.Fori(1, GROUPS) as gr:
                group(gr, False)
            pe.wait_ge(mask_ready, 1)
            for n, w in enumerate((below, ones)):
                last = nc.tensor.matmul(rank_ps[:, P * n:P * (n + 1)], w[:, :],
                                        mask[:, :, :].rearrange("p i e -> p (i e)"), start=True, stop=True)
            last.then_inc(rank_ready, 1)
            pe.wait_ge(entries_ready, TOP + 2)
            for j in range(TOP * TILES):
                last = nc.tensor.matmul(rank_ps[:, 2 * P:2 * P + 2 * BLOCKS], row_hot[:, j, :],
                                        entries[:, j, :, :].rearrange("p w b -> p (w b)"),
                                        start=(j == 0), stop=(j == TOP * TILES - 1))
            last.then_inc(table_summed, 1)

            def turn_rows(b):
                pe.wait_ge(gathered, 16 * (b + 1))
                for kt in range(KT):
                    last = nc.tensor.transpose(t_ps[:, 0, P * kt:P * (kt + 1)], rows[:, P * kt:P * (kt + 1)],
                                               ident[:, :])
                last.then_inc(t_ready, 1)

            def down(b, par):
                pe.wait_ge(gt_done, b + 1)
                for ft in range(FT):
                    for gt, w in ((gt_hi, w2_hi), (gt_hi, w2_lo), (gt_lo, w2_hi)):
                        last = nc.tensor.matmul(y_ps[:, :], gt[:, ft, :], w[par][:, ft, :],
                                                start=(ft == 0 and gt is gt_hi and w is w2_hi),
                                                stop=(ft == FT - 1 and gt is gt_lo))
                last.then_inc(y_ready, 1)

            def step(b, e, par, opens, started, has_next):
                if opens:
                    pe.wait_ge(w13_cut, e + 1)
                    pe.wait_ge(w2_cut, e + 1)
                pe.wait_ge(xb_done, b + 1)
                for kt in range(KT):
                    for x, w in ((xb_hi, w13_hi), (xb_hi, w13_lo), (xb_lo, w13_hi)):
                        last = nc.tensor.matmul(h_ps[:, :], x[:, kt, :], w[par][:, kt, :],
                                                start=(kt == 0 and x is xb_hi and w is w13_hi),
                                                stop=(kt == KT - 1 and x is xb_lo))
                last.then_inc(h_ready, 1)
                turn_rows(b + 1)
                if started:
                    down(b - 1, 1 - par if opens else par)
                pe.wait_ge(g_done, b + 1)
                for ft in range(FT):
                    last = nc.tensor.transpose(gt_ps[:, ft, :], g[:, P * ft:P * (ft + 1)], ident[:, :])
                last.then_inc(gt_ready, 1)

            pe.wait_ge(spans_ready, 3)
            turn_rows(0)
            over_blocks(pe, step)
            down(load_tail(pe) + 1, 1)


def xattn_moe(nc, x, ctx_in, wq, bq, wk, bk, wv, bv, wo, bo, wg, w1, w3, w2, bias, out):
    q_scratch = nc.dram_tensor("q_scratch", [B, 2, PARTS, HD, H, T], BF16, kind="Internal").ap()
    o_scratch = nc.dram_tensor("o_scratch", [B, UNITS, P, T], F32, kind="Internal").ap()
    r_scratch = nc.dram_tensor("r_scratch", [B, H, T], F32, kind="Internal").ap()
    xn_rows = nc.dram_tensor("xn_rows", [B, C, T], F32, kind="Internal").ap()
    with nc.sbuf_tensor("x1", [P, B, CT, T], F32) as x1:
        attention(nc, x, ctx_in, wq, bq, wk, bk, wv, bv, wo, bo, x1, q_scratch, o_scratch, r_scratch)
        experts(nc, x1, xn_rows, wg, w1, w3, w2, bias, out)


def kernel(x, ctx_2048, L0_xattn_Wq, L0_xattn_bq, L0_xattn_Wk, L0_xattn_bk, L0_xattn_Wv, L0_xattn_bv,
           L0_xattn_Wo, L0_xattn_bo, L0_ffn_Wg, L0_ffn_W1, L0_ffn_W2, L0_ffn_W3, L0_ffn_bias):
    import numpy as np
    import concourse.bacc as bacc
    from concourse.bass_utils import run_bass_kernel_spmd

    def by_channel(w):
        w = np.asarray(w)
        return np.swapaxes(w.reshape(H, HD, *w.shape[1:]), 0, 1).reshape(w.shape)

    def column(v):
        return np.asarray(v).reshape(CT, P).T

    arrays = {
        "x": x, "ctx": ctx_2048,
        "wq": by_channel(L0_xattn_Wq).T, "bq": column(by_channel(L0_xattn_bq)),
        "wk": by_channel(L0_xattn_Wk).T, "bk": column(by_channel(L0_xattn_bk)),
        "wv": np.asarray(L0_xattn_Wv).T, "bv": column(L0_xattn_bv),
        "wo": np.asarray(L0_xattn_Wo).T, "bo": column(L0_xattn_bo),
        "wg": np.asarray(L0_ffn_Wg).T,
        "w1": np.swapaxes(np.asarray(L0_ffn_W1), 1, 2), "w3": np.swapaxes(np.asarray(L0_ffn_W3), 1, 2),
        "w2": np.swapaxes(np.asarray(L0_ffn_W2), 1, 2), "bias": np.asarray(L0_ffn_bias).reshape(1, E),
    }
    arrays = {f"in_{k}": np.ascontiguousarray(v) for k, v in arrays.items()}
    nc = bacc.Bacc("TRN2", target_bir_lowering=False, num_devices=1)
    args = [nc.dram_tensor(k, v.shape, mybir.dt.from_np(v.dtype), kind="ExternalInput").ap() for k, v in arrays.items()]
    out = nc.dram_tensor("out", [B, C, T], F32, kind="ExternalOutput").ap()
    xattn_moe(nc, *args, out)
    return run_bass_kernel_spmd(nc, [arrays], core_ids=[0]).results[0]["out"]
```

```python
import concourse.bass as bass
from concourse import mybir
from contextlib import ExitStack

F32 = mybir.dt.float32
F32R = mybir.dt.float32r
BF16 = mybir.dt.bfloat16
U32 = mybir.dt.uint32
ALU = mybir.AluOpType
ACT = mybir.ActivationFunctionType
AX = mybir.AxisListType

P = 128
B, C, T = 8, 256, 512
H, HD = 16, 16
CT = C // P
TT = T // P
UNITS, UH = 4, 4
SLOTS = UH * TT
PARTS = 3
QROWS = 6 * HD
KROWS = QROWS + PARTS
VW = 32
K_GROUPS = ((0, 3), (3, 2), (5, 1))
Q_GROUPS = ((0, 0, 3), (3, 1, 2), (5, 2, 1))
STACK_DMAS = len(K_GROUPS) + len(Q_GROUPS)
LAG = UNITS + 1
SCALE = 1.0 / HD ** 0.5
EPS = 1e-5
E, FF = 8, 256
KT = T // P
FT = FF // P
TOKENS = B * C
TILES = TOKENS // P
TOP = 2
WG_COLS = 32
MIN_BLOCKS = 1
BLOCKS = TOP * TOKENS // P + MIN_BLOCKS * E
TABLE = BLOCKS + 1
SHIFT = P.bit_length() - 1
PLANES = 3
CHUNKS = 4
CHUNK = TOP * TILES // CHUNKS
TOP_STEPS = 4


def attention(nc, x, ctx_in, wq, bq, wk, bk, wv, bv, wo, bo, wg, bias, x1, route, top_at, xn_stored, x1_stored,
              q_scratch, o_scratch, r_scratch, xn_rows, out):
    es = ExitStack()
    with es:
        def sb(name, shape, dt):
            return es.enter_context(nc.sbuf_tensor(name, shape, dt))

        def ps(name, shape):
            return es.enter_context(nc.psum_tensor(name, shape, F32))

        def sem(name):
            return es.enter_context(nc.semaphore(name))

        w_sb = {name: sb(f"{name}_sb", [P, CT, C], F32) for name in ("wq", "wk", "wv", "wo")}
        vecs = sb("vecs", [P, 4, CT], F32)
        bq_sb, bk_sb, bv_sb, bo_sb = (vecs[:, i, :] for i in range(4))
        bout = sb("bout", [P, CT], F32)
        ident = sb("ident", [P, P], F32)
        minus_half = sb("minus_half", [P, CT], F32)
        ctx_sb = sb("ctx_sb", [P, 2, CT, T], F32)
        xn = sb("xn", [P, CT, T], F32)
        stats = sb("stats", [P, CT, 6], F32)
        mean_var = sb("mean_var", [P, CT, 2], F32)
        var_eps = sb("var_eps", [P, CT], F32)
        pace = sb("pace", [P, 1], F32)
        rstd = sb("rstd", [P, CT], F32)
        qk = sb("qk", [P, 2, CT * T], F32)
        parts = sb("parts", [P, 2, PARTS, CT * T], BF16)
        qs = [sb(f"qs{i}", [P, H, T], BF16) for i in range(2)]
        ks = [sb(f"ks{i}", [P, H, T], BF16) for i in range(2)]
        v_sb = [sb(f"v{i}", [P, TT, H, VW], F32) for i in range(2)]
        neg_max = [sb(f"neg_max{i}", [P, H * TT], F32) for i in range(2)]
        m_rest = sb("m_rest", [H * TT, 2, P], F32)
        m_parts = sb("m_parts", [H * TT, PARTS, P], BF16)
        probs = sb("probs", [P, TT, UH, T], F32)
        o_sb = sb("o_sb", [P, 2, T], F32)
        den = sb("den", [P, 64], F32)
        rden = sb("rden", [P, 64], F32)
        o_heads = sb("o_heads", [P, CT, T], F32)
        r_heads = sb("r_heads", [P, CT, T], F32)
        o_norm = sb("o_norm", [P, CT, T], F32)
        stats_e = sb("stats_e", [P, CT, 6], F32)
        mean_var_e = sb("mean_var_e", [P, CT, 2], F32)
        var_eps_e = sb("var_eps_e", [P, CT], F32)
        rstd_e = sb("rstd_e", [P, CT], F32)
        wg_sb = sb("wg_sb", [P, KT, WG_COLS], F32)
        bias_row = sb("bias_row", [P, E], F32)
        logits = sb("logits", [P, CT, E], F32)
        exp_neg = sb("exp_neg", [P, CT, E], F32)
        exp_neg_1 = sb("exp_neg_1", [P, CT, E], F32)
        score = sb("score", [P, CT, E], F32)
        top = sb("top", [P, CT, E], F32)
        x1n = ctx_sb
        x1t = qk[:, 0, :].rearrange("p (k t) -> p k t", k=KT)
        logits_t = xn[:, 0, 0:C]

        st_ps = [ps(f"st_ps{i}", [P, T]) for i in range(2)]
        s_ps = [ps(f"s_ps{i}", [P, 2, T]) for i in range(2)]
        o_ps = ps("o_ps", [P, T])
        misc = ps("misc", [P, T])

        w_loaded = {name: sem(f"{name}_loaded") for name in ("wq", "wk", "wv", "wo")}
        vecs_loaded = sem("vecs_loaded")
        x_loaded = [sem(f"x_loaded{i}") for i in range(2)]
        ctx_loaded = [sem(f"ctx_loaded{i}") for i in range(2)]
        const_ready = sem("const_ready")
        ident_zero = sem("ident_zero")
        ident_ready = sem("ident_ready")
        stats_ready = sem("stats_ready")
        mv_ready = sem("mv_ready")
        eps_added = sem("eps_added")
        rstd_ready = sem("rstd_ready")
        xn_ready = sem("xn_ready")
        qk_ready, qk_done = sem("qk_ready"), sem("qk_done")
        part1, rest1, part2, part3 = sem("part1"), sem("rest1"), sem("part2"), sem("part3")
        parts_stored = [sem(f"parts_stored{i}") for i in range(2)]
        stack_loaded = [sem(f"stack_loaded{u}") for u in range(UNITS)]
        v_ready, v_done = sem("v_ready"), sem("v_done")
        s_ready, max_done = sem("s_ready"), sem("max_done")
        m_ready, m_part1, m_rest1, m_part2, m_rest2, m_done = (
            sem(n) for n in ("m_ready", "m_part1", "m_rest1", "m_part2", "m_rest2", "m_done"))
        m_loaded = sem("m_loaded")
        st_ready, exp_done = sem("st_ready"), sem("exp_done")
        pv_done, o_done = sem("pv_done"), sem("o_done")
        o_stored = [sem(f"o_stored{i}") for i in range(2)]
        den_loaded, rden_ready, rden_stored, heads_loaded = (
            sem(n) for n in ("den_loaded", "rden_ready", "rden_stored", "heads_loaded"))
        on_ready = sem("on_ready")
        wo_ready, wo_done = sem("wo_ready"), sem("wo_done")
        wg_zero, route_loaded = sem("wg_zero"), sem("route_loaded")
        x1_stats_ready, x1_mv_ready, x1_eps_added, x1_rstd_ready, x1n_ready = (
            sem(n) for n in ("x1_stats_ready", "x1_mv_ready", "x1_eps_added", "x1_rstd_ready", "x1n_ready"))
        x1t_ready, x1t_done, logits_t_ready, logits_t_done = (
            sem(n) for n in ("x1t_ready", "x1t_done", "logits_t_ready", "logits_t_done"))
        logits_ready, logits_done, exp_neg_done, top_steps = (
            sem(n) for n in ("logits_ready", "logits_done", "exp_neg_done", "top_steps"))

        def x1_at(n, ct):
            v = x1[:, bass.ds(n, 1), ct, :]
            return v.rearrange("p o t -> p (o t)")

        def iterate(engine, step):
            for n in (0, 1):
                for u in range(UNITS):
                    step(n, n % 2, u, n // 2)
            with engine.Fori(1, 3) as i:
                for par in range(2):
                    for u in range(UNITS):
                        step(2 * i + par, par, u, i)
            for n in (6, 7, 8, 9):
                for u in range(UNITS):
                    step(n, n % 2, u, n // 2)

        def out_bank(m, ot):
            return st_ps[ot][:, :] if isinstance(m, int) and m == B - 1 else misc[:, :]

        def qk_bank(m, j):
            return s_ps[j // 2][:, j % 2, :] if isinstance(m, int) and m == 0 else misc[:, :]

        def late(n, first):
            return n >= first if isinstance(n, int) else 2 >= first

        def early(n, last):
            return n <= last if isinstance(n, int) else 5 <= last

        def routes(n, u, ahead=0):
            f = UNITS * (n - B) + u + ahead if isinstance(n, int) else -1
            return f if 0 <= f < B - 1 else None

        def unit_runs(n, u):
            return not isinstance(n, int) or 0 <= UNITS * n + u - LAG < UNITS * B

        block = es.enter_context(nc.Block())

        @block.sync
        def _(sp):
            def load_x(m, par):
                sp.dma_start(x1[:, bass.ds(m, 1), :, :].rearrange("p o c t -> p (o c) t"),
                             x[bass.ds(m, 1)].rearrange("o (c p) t -> p (o c) t", p=P)).then_inc(x_loaded[par], 16)

            def load_ctx(m, par):
                sp.dma_start(ctx_sb[:, par, :, :],
                             ctx_in[bass.ds(m, 1)].rearrange("o (c p) t -> p (o c) t", p=P)).then_inc(ctx_loaded[par], 16)

            def store_parts(m, par):
                sp.wait_ge(part3, m + 1)
                sp.dma_start(q_scratch[bass.ds(m, 1)].rearrange("o w g (c k) h t -> (k h) (o w g c) t", c=CT),
                             parts[:, :, :, :].rearrange("p w g (c t) -> p (w g c) t", c=CT)
                             ).then_inc(parts_stored[par], 16)

            rows = q_scratch.rearrange("n w g k h t -> n w (g k) h t")

            def load_stack(m, par, i, u):
                if late(m, 2):
                    sp.wait_ge(pv_done, UNITS * TT * (m - 2) + TT * (u + 1))
                if u == 0:
                    sp.wait_ge(parts_stored[par], 16 * i + 16)
                heads = slice(UH * u, UH * (u + 1))

                for g, count in K_GROUPS:
                    src = rows[bass.ds(m, 1), 1, 0:HD * count, heads, :]
                    sp.dma_start(ks[par][HD * g:HD * (g + count), heads, :],
                                 src.rearrange("o r h t -> (o r) h t")).then_inc(stack_loaded[u], 16)
                for g, part, count in Q_GROUPS:
                    src = rows[bass.ds(m, 1), 0, HD * part:HD * (part + 1), heads, :]
                    sp.dma_start(qs[par][HD * g:HD * (g + count), heads, :],
                                 src.rearrange("o r h t -> o r (h t)").to_broadcast([count, HD, UH * T])
                                 ).then_inc(stack_loaded[u], 16)

            def load_m_rows(m, par):
                sp.wait_ge(m_done, m + 1)
                for g in range(PARTS):
                    sp.dma_start(qs[par][QROWS + g:QROWS + g + 1, :, :].rearrange("o h (a t) -> o (h a) t", a=TT),
                                 m_parts[:, g, :]).then_inc(m_loaded, 16)

            def store_o(n, u):
                tc = UNITS * n + u - LAG - 1
                m, mu = (n - 1, u - 2) if u >= 2 else (n - 2, u + 2)
                sp.wait_ge(o_done, tc + 1)
                sp.dma_start(o_scratch[bass.ds(m, 1), mu].rearrange("o r t -> (o r) t"),
                             o_sb[:, mu % 2, :]).then_inc(o_stored[mu % 2], 16)

            def load_den(m):
                for i in range(2):
                    sp.wait_ge(o_stored[i], 32 * (m + 1))
                den_rows = o_scratch.rearrange("n u (j r) t -> n (u j) r t", r=VW)
                sp.dma_start(den[:, :], den_rows[bass.ds(m, 1), :, HD, :].rearrange("o h t -> (o h) t")
                             ).then_inc(den_loaded, 16)
                for ct in range(CT):
                    src = den_rows[bass.ds(m, 1), 8 * ct:8 * (ct + 1), 0:HD, :]
                    sp.dma_start(o_heads[:, ct, :], src.rearrange("o h r t -> (o h) r t")).then_inc(heads_loaded, 16)
                sp.wait_ge(rden_ready, m + 1)
                sp.dma_start(r_scratch[bass.ds(m, 1)].rearrange("o h (a t) -> (o h a) t", a=8),
                             rden[:, :]).then_inc(rden_stored, 16)
                sp.wait_ge(rden_stored, 16 * (m + 1))
                for ct in range(CT):
                    src = r_scratch[bass.ds(m, 1), 8 * ct:8 * (ct + 1), :].rearrange("o (h r) t -> (o h) r t", r=1)
                    sp.dma_start(r_heads[:, ct, :], src.to_broadcast([8, HD, T])).then_inc(heads_loaded, 16)

            load_x(0, 0)
            for name, src in (("wq", wq), ("wk", wk), ("wv", wv), ("wo", wo)):
                sp.dma_start(w_sb[name][:, :, :], src.rearrange("(c p) o -> p c o", p=P)).then_inc(w_loaded[name], 16)
                if name == "wq":
                    load_ctx(0, 0)
                    for vec, v in enumerate((bq, bk, bv, bo)):
                        sp.dma_start(vecs[:, vec, :], v.rearrange("p c -> p c")).then_inc(vecs_loaded, 16)
            load_x(1, 1)
            load_ctx(1, 1)
            sp.wait_ge(wg_zero, 1)
            sp.dma_start(wg_sb[:, :, 0:E], wg.rearrange("(k p) e -> p k e", p=P)).then_inc(route_loaded, 16)
            sp.dma_start(bias_row[:, :], bias.to_broadcast([P, E])).then_inc(route_loaded, 16)
            store_parts(0, 0)
            load_stack(0, 0, 0, 0)
            load_stack(0, 0, 0, 1)

            def store_x1(f):
                sp.wait_ge(wo_done, 1 + CT * (f + 1))
                sp.dma_start(out[f].rearrange("(c p) t -> p c t", p=P), x1[:, f, :, :]).then_inc(x1_stored, 16)

            def store_x1n(f):
                sp.wait_ge(x1n_ready, CT * (f + 1))
                sp.dma_start(xn_rows[f].rearrange("(c p) t -> p c t", p=P), x1n[:, f % 2, :, :]
                             ).then_inc(xn_stored[f % 2], 16)

            def step(n, par, u, i):
                f = routes(n, u)
                if unit_runs(n, u - 1) and u >= 0:
                    store_o(n, u)
                if f is not None:
                    store_x1(f)
                    if f:
                        store_x1n(f - 1)
                if u == 0 and early(n, 5):
                    load_x(n + 2, par)
                if u == 2 and early(n, 6):
                    load_stack(n + 1, 1 - par, i + par, 0)
                if u == 3 and early(n, 6):
                    load_stack(n + 1, 1 - par, i + par, 1)
                if u == 0 and early(n, 7):
                    load_stack(n, par, i, 2)
                if u == 1 and early(n, 7):
                    load_stack(n, par, i, 3)
                if u == 1 and late(n, 2):
                    load_den(n - 2)
                if u == 1 and early(n, 6):
                    store_parts(n + 1, 1 - par)
                if u == 0 and late(n, 1) and early(n, 8):
                    load_m_rows(n - 1, 1 - par)
                if u == 3 and early(n, 5):
                    sp.wait_ge(v_ready, 2 * (n + 1))
                    load_ctx(n + 2, par)

            iterate(sp, step)
            for f in (B - 2, B - 1):
                store_x1n(f)

        @block.gpsimd
        def _(pool):
            nc.gpsimd.memset(minus_half[:, :], -0.5)
            nc.gpsimd.memset(ident[:, :], 0.0).then_inc(ident_zero, 1)
            nc.gpsimd.memset(wg_sb[:, :, :], 0.0).then_inc(wg_zero, 1)
            pool.wait_ge(ident_zero, 1)
            nc.gpsimd.affine_select(out=ident[:, :], in_=ident[:, :], compare_op=ALU.not_equal, fill=1.0, base=0,
                                    pattern=[[-1, P]], channel_multiplier=1).then_inc(ident_ready, 1)
            for buf in v_sb:
                nc.gpsimd.memset(buf[:, :, :, HD:VW], 1.0).then_inc(const_ready, 1)

            def norm_scale(m):
                pool.wait_ge(eps_added, m + 1)
                nc.gpsimd.tensor_tensor(rstd[:, :], var_eps[:, :], minus_half[:, :], ALU.pow).then_inc(rstd_ready, 1)

            def split(m):
                pool.wait_ge(part1, m + 1)
                nc.gpsimd.tensor_tensor(qk[:, :, :], qk[:, :, :], parts[:, :, 0, :], ALU.subtract).then_inc(rest1, 1)
                pool.wait_ge(part2, m + 1)
                nc.gpsimd.tensor_tensor(parts[:, :, 2, :], qk[:, :, :], parts[:, :, 1, :],
                                        ALU.subtract).then_inc(part3, 1)

            def normalize(m):
                pool.wait_ge(heads_loaded, 2 * CT * 16 * (m + 1))
                pool.wait_ge(wo_ready, CT * m + 1)
                nc.gpsimd.tensor_tensor(o_norm[:, :, :], o_heads[:, :, :], r_heads[:, :, :],
                                        ALU.mult).then_inc(on_ready, 1)

            norm_scale(0)
            norm_scale(1)

            def x1_scale(f):
                pool.wait_ge(x1_eps_added, f + 1)
                nc.gpsimd.tensor_tensor(rstd_e[:, :], var_eps_e[:, :], minus_half[:, :], ALU.pow
                                        ).then_inc(x1_rstd_ready, 1)

            def step(n, par, u, i):
                if routes(n, u, 1) is not None:
                    x1_scale(routes(n, u, 1))
                if u == 1 and early(n, 6):
                    split(n + 1)
                if u == 2 and late(n, 2) and early(n, B):
                    normalize(n - 2)
                if u == 2 and early(n, 5):
                    norm_scale(n + 2)

            iterate(pool, step)
            x1_scale(B - 1)

        @block.scalar
        def _(act):
            def evacuate_qk(m, j):
                act.wait_ge(qk_ready, 4 * m + j + 1)
                if j == 0 and late(m, 1):
                    act.wait_ge(part3, m)
                bias = (bq_sb, bk_sb)[j // CT][:, j % CT:j % CT + 1]
                nc.scalar.activation(qk[:, j // CT, T * (j % CT):T * (j % CT + 1)], qk_bank(m, j), ACT.Identity,
                                     bias=bias).then_inc(qk_done, 1)

            def evacuate_v(m, par, j):
                act.wait_ge(v_ready, 2 * m + j + 1)
                if j == 0 and late(m, 2):
                    act.wait_ge(pv_done, UNITS * TT * (m - 1))
                nc.scalar.copy(v_sb[par][:, 2 * j:2 * j + 2, :, 0:HD],
                               misc[:, :].rearrange("p (s h k) -> p s h k", s=2, h=H)).then_inc(v_done, 1)

            def evacuate_o(tc, n, u):
                act.wait_ge(pv_done, TT * (tc + 1))
                if late(tc, 2):
                    act.wait_ge(o_stored[u % 2], 16 * (2 * n + (u - 6) // 2))
                nc.scalar.copy(o_sb[:, u % 2, :], o_ps[:, :]).then_inc(o_done, 1)

            def route_exp(f):
                act.wait_ge(logits_done, f + 1)
                nc.scalar.activation(exp_neg[:, :, :], logits[:, :, :], ACT.Exp, scale=-1.0).then_inc(exp_neg_done, 1)

            act.wait_ge(vecs_loaded, 4 * 16)
            for j in range(2 * CT):
                evacuate_qk(0, j)

            def step(n, par, u, i):
                tc = UNITS * n + u - LAG
                for pair in range(SLOTS // 2):
                    for slot in (2 * pair, 2 * pair + 1):
                        if unit_runs(n, u):
                            act.wait_ge(st_ready, SLOTS * tc + slot + 1)
                            if slot % UH == 0 and late(tc, 1):
                                act.wait_ge(pv_done, TT * (tc - 1) + slot // UH + 1)
                            nc.scalar.activation(probs[:, slot // UH, slot % UH, :], st_ps[slot % 2][:, :], ACT.Exp,
                                                 scale=SCALE).then_inc(exp_done, 1)
                    if pair == 2 and unit_runs(n, u - 1):
                        evacuate_o(tc - 1, n, u)
                    if early(n, 6) and u == 0 and pair in (2, 4, 6):
                        evacuate_qk(n + 1, pair // 2 - 1)
                    if early(n, 6) and u == 1 and pair == 2:
                        evacuate_qk(n + 1, 3)
                    if early(n, 7) and u == 2 and pair in (2, 5):
                        evacuate_v(n, par, pair // 4)

                    if pair == 1 and routes(n, u, -1) is not None:
                        route_exp(routes(n, u, -1))

            iterate(act, step)
            route_exp(B - 1)

        @block.vector
        def _(dve):
            def norm_stats(m, par, i, ct):
                dve.wait_ge(x_loaded[par], 16 * i + 16)
                nc.vector.bn_stats(stats[:, ct, :], x1_at(m, ct)).then_inc(stats_ready, 1)

            def norm_sums(m):
                dve.wait_ge(stats_ready, CT * (m + 1))
                nc.vector.memset(pace[:, :], 0.0)
                for ct in range(CT):
                    nc.vector.bn_aggr(mean_var[:, ct, :], stats[:, ct, :]).then_inc(mv_ready, 1)
                dve.wait_ge(mv_ready, CT * (m + 1))
                nc.vector.tensor_scalar(var_eps[:, :], mean_var[:, :, 1], EPS, None, ALU.add).then_inc(eps_added, 1)

            def norm_apply(m, ct):
                if ct == 0:
                    dve.wait_ge(rstd_ready, m + 1)
                    if late(m, 1):
                        dve.wait_ge(qk_ready, 4 * (m - 1) + CT)
                nc.vector.tensor_scalar(xn[:, ct, :], x1_at(m, ct), mean_var[:, ct, 0:1], rstd[:, ct:ct + 1],
                                        ALU.subtract, ALU.mult).then_inc(xn_ready, 1)

            def round_first(m, par, i):
                dve.wait_ge(qk_done, 4 * (m + 1))
                if late(m, 1):
                    dve.wait_ge(parts_stored[1 - par], 16 * (i + par))
                nc.vector.tensor_copy(parts[:, :, 0, :], qk[:, :, :]).then_inc(part1, 1)

            def round_second(m):
                dve.wait_ge(rest1, m + 1)
                nc.vector.tensor_copy(parts[:, :, 1, :], qk[:, :, :]).then_inc(part2, 1)

            def split_max(m):
                dve.wait_ge(m_ready, m + 1)
                if late(m, 1):
                    dve.wait_ge(m_loaded, 16 * PARTS * m)
                mt = misc[0:H * TT, 0:P]
                nc.vector.tensor_copy(m_parts[:, 0, :], mt).then_inc(m_part1, 1)
                dve.wait_ge(m_part1, m + 1)
                nc.vector.tensor_tensor(m_rest[:, 0, :], mt, m_parts[:, 0, :], ALU.subtract).then_inc(m_rest1, 1)
                dve.wait_ge(m_rest1, m + 1)
                nc.vector.tensor_copy(m_parts[:, 1, :], m_rest[:, 0, :]).then_inc(m_part2, 1)
                dve.wait_ge(m_part2, m + 1)
                nc.vector.tensor_tensor(m_parts[:, 2, :], m_rest[:, 0, :], m_parts[:, 1, :],
                                        ALU.subtract).then_inc(m_done, 1)

            def add_residual(m, ot):
                dve.wait_ge(wo_ready, 1 + CT * m + ot + 1)
                nc.vector.scalar_tensor_tensor(out=x1_at(m, ot), in0=out_bank(m, ot), scalar=bout[:, ot:ot + 1],
                                               in1=x1_at(m, ot), op0=ALU.add, op1=ALU.add).then_inc(wo_done, 1)

            def x1_norm(f):
                for ct in range(CT):
                    dve.wait_ge(wo_done, 1 + CT * f + ct + 1)
                    nc.vector.bn_stats(stats_e[:, ct, :], x1[:, f, ct, :]).then_inc(x1_stats_ready, 1)
                dve.wait_ge(x1_stats_ready, CT * (f + 1))
                for ct in range(CT):
                    nc.vector.bn_aggr(mean_var_e[:, ct, :], stats_e[:, ct, :]).then_inc(x1_mv_ready, 1)
                dve.wait_ge(x1_mv_ready, CT * (f + 1))
                nc.vector.tensor_scalar(var_eps_e[:, :], mean_var_e[:, :, 1], EPS, None, ALU.add
                                        ).then_inc(x1_eps_added, 1)
                dve.wait_ge(x1_rstd_ready, f + 1)
                if f == 0:
                    dve.wait_ge(v_ready, 2 * B)
                    dve.wait_ge(part3, B)
                if f >= 2:
                    dve.wait_ge(xn_stored[f % 2], 16 * (f // 2))
                for ct in range(CT):
                    nc.vector.tensor_scalar(x1n[:, f % 2, ct, :], x1[:, f, ct, :], mean_var_e[:, ct, 0:1],
                                            rstd_e[:, ct:ct + 1], ALU.subtract, ALU.mult).then_inc(x1n_ready, 1)

            def take_x1t(f):
                for ct in range(CT):
                    dve.wait_ge(x1t_ready, CT * f + ct + 1)
                    nc.vector.tensor_copy(x1t[:, :, P * ct:P * (ct + 1)],
                                          s_ps[ct][:, 0, :].rearrange("p (k t) -> p k t", k=KT)).then_inc(x1t_done, 1)

            def take_logits_t(f):
                dve.wait_ge(logits_t_ready, f + 1)
                nc.vector.tensor_copy(logits_t, s_ps[0][:, 0, 0:C]).then_inc(logits_t_done, 1)

            def take_logits(f):
                dve.wait_ge(logits_ready, f + 1)
                parts_of = s_ps[1][:, 0, 0:C].rearrange("p (c k e) -> p c k e", c=CT, k=KT)[:, :, :, 0:E]
                nc.vector.tensor_reduce(logits[:, :, :], parts_of.rearrange("p c k e -> p c e k"), AX.X, ALU.add
                                        ).then_inc(logits_done, 1)

            def take_top(f):
                rows = slice(CT * f, CT * (f + 1))
                dve.wait_ge(exp_neg_done, f + 1)
                nc.vector.tensor_scalar(exp_neg_1[:, :, :], exp_neg[:, :, :], 1.0, None, ALU.add
                                        ).then_inc(top_steps, 1)
                dve.wait_ge(top_steps, TOP_STEPS * f + 1)
                nc.vector.reciprocal(route[:, rows, :], exp_neg_1[:, :, :]).then_inc(top_steps, 1)
                dve.wait_ge(top_steps, TOP_STEPS * f + 2)
                nc.vector.tensor_tensor(score[:, :, :], route[:, rows, :],
                                        bias_row[:, :].rearrange("p (o e) -> p o e", o=1).to_broadcast([P, CT, E]),
                                        ALU.add).then_inc(top_steps, 1)
                dve.wait_ge(top_steps, TOP_STEPS * f + 3)
                for ct in range(CT):
                    last = nc.vector.max(top[:, ct, :], score[:, ct, :])
                last.then_inc(top_steps, 1)
                dve.wait_ge(top_steps, TOP_STEPS * (f + 1))
                for ct in range(CT):
                    nc.vector.max_index(top_at[:, CT * f + ct, :], top[:, ct, :], score[:, ct, :])

            def set_ones(buf):
                nc.vector.memset(buf[QROWS:KROWS, :, :], 1.0).then_inc(const_ready, 1)

            for m in (0, 1):
                for ct in range(CT):
                    norm_stats(m, m, 0, ct)
                norm_sums(m)
                if m == 0:
                    for ct in range(CT):
                        norm_apply(0, ct)
                    set_ones(ks[0])
            for ct in range(CT):
                norm_apply(1, ct)
            round_first(0, 0, 0)
            dve.wait_ge(part1, 1)
            nc.vector.tensor_tensor(qk[:, :, :], qk[:, :, :], parts[:, :, 0, :], ALU.subtract).then_inc(rest1, 1)
            round_second(0)
            dve.wait_ge(part2, 1)
            nc.vector.tensor_tensor(parts[:, :, 2, :], qk[:, :, :], parts[:, :, 1, :], ALU.subtract).then_inc(part3, 1)
            dve.wait_ge(vecs_loaded, 4 * 16)
            dve.wait_ge(wo_ready, 1)
            nc.vector.tensor_tensor(bout[:, :], misc[:, 0:CT], bo_sb, ALU.add).then_inc(wo_done, 1)
            set_ones(ks[1])

            def step(n, par, u, i):
                f = routes(n, u)
                if f == 0:
                    dve.wait_ge(route_loaded, 32)
                if early(n, 7) and u == 0 and late(n, 2):
                    dve.wait_ge(m_ready, n - 1)
                for slot in range(SLOTS):
                    if early(n, 7) and slot % 2:
                        pair = slot // 2
                        dve.wait_ge(s_ready, (SLOTS // 2) * (UNITS * n + u) + pair + 1)
                        col = SLOTS * u + 2 * pair
                        nc.vector.tensor_reduce(neg_max[par][:, col:col + 2], s_ps[pair % 2][:, :, :], AX.X, ALU.max,
                                                negate=True).then_inc(max_done, 1)
                    if u == 0 and slot == 3 and late(n, 1) and early(n, 8):
                        split_max(n - 1)
                    if u == 1 and early(n, 6):
                        if slot == 7:
                            round_first(n + 1, 1 - par, i + par)
                        if slot == 13:
                            round_second(n + 1)
                    if u == 2 and slot == (2 if early(n, 7) else 0) and late(n, 2):
                        dve.wait_ge(den_loaded, 16 * (n - 1))
                        nc.vector.reciprocal(rden[:, :], den[:, :]).then_inc(rden_ready, 1)
                    if u == 2 and early(n, 5):
                        if slot in (7, 11):
                            norm_stats(n + 2, par, i + 1, slot // 11)
                        if slot == 13:
                            norm_sums(n + 2)
                    if u == 3 and early(n, 5) and slot in (3, 5):
                        norm_apply(n + 2, slot // 5)
                    if u == 3 and slot == 5 and not early(n, B):
                        dve.wait_ge(heads_loaded, 2 * CT * 16 * B)
                        dve.wait_ge(wo_ready, CT * (B - 1) + 1)
                        nc.vector.tensor_tensor(o_norm[:, :, :], o_heads[:, :, :], r_heads[:, :, :],
                                                ALU.mult).then_inc(on_ready, 1)
                    if u == 3 and slot in (7, 13) and late(n, 2):
                        add_residual(n - 2, slot // 13)
                    if f is not None:
                        if slot == 6:
                            take_x1t(f)
                        if slot == 10:
                            take_logits_t(f)
                        if slot == 11 and routes(n, u, 1) is not None:
                            x1_norm(f + 1)
                        if slot == 14:
                            take_logits(f)
                    if slot == 4 and routes(n, u, -1) is not None:
                        take_top(routes(n, u, -1))

                if routes(n, u, 1) == 0:
                    x1_norm(0)

            iterate(dve, step)
            for stage in (x1_norm, take_x1t, take_logits_t, take_logits, take_top):
                stage(B - 1)

        @block.tensor
        def _(pe):
            def project_qk(m, par, i, j):
                which, ct_out = j // CT, j % CT
                w, src = (w_sb["wq"], xn) if which == 0 else (w_sb["wk"], ctx_sb[:, par])
                if j == 0:
                    pe.wait_ge(xn_ready, CT * (m + 1))
                    if late(m, 1):
                        pe.wait_ge(qk_done, 4 * m)
                    if late(m, 2):
                        pe.wait_ge(m_rest1, m - 1)
                if j == CT:
                    pe.wait_ge(ctx_loaded[par], 16 * i + 16)
                if j and late(m, 1):
                    pe.wait_ge(qk_done, 4 * m + j)
                for ct in range(CT):
                    last = nc.tensor.matmul(qk_bank(m, j), w[:, ct, P * ct_out:P * (ct_out + 1)], src[:, ct, :],
                                            start=(ct == 0), stop=(ct == CT - 1))
                last.then_inc(qk_ready, 1)

            def project_v(m, par, j):
                if j == 0:
                    if early(m, 6):
                        pe.wait_ge(qk_done, 4 * (m + 2))
                    else:
                        pe.wait_ge(m_rest1, m)
                else:
                    pe.wait_ge(v_done, 2 * m + 1)
                for half in range(2):
                    s0 = P * (2 * j + half)
                    for ct in range(CT):
                        last = nc.tensor.matmul(misc[:, C * half:C * (half + 1)], ctx_sb[:, par, ct, s0:s0 + P],
                                                w_sb["wv"][:, ct, :], start=(ct == 0), stop=(ct == CT - 1))
                last.then_inc(v_ready, 1)

            def project_out(m, ot):
                if ot == 0:
                    pe.wait_ge(on_ready, m + 1)
                    if early(m, 5):
                        pe.wait_ge(v_done, 2 * (m + 3))
                    else:
                        pe.wait_ge(m_rest1, B)
                if ot == 0 or not (isinstance(m, int) and m == B - 1):
                    pe.wait_ge(wo_done, 1 + CT * m + ot)
                for ct in range(CT):
                    last = nc.tensor.matmul(out_bank(m, ot), w_sb["wo"][:, ct, P * ot:P * (ot + 1)], o_norm[:, ct, :],
                                            start=(ct == 0), stop=(ct == CT - 1))
                last.then_inc(wo_ready, 1)

            def wait_to_transpose(m):
                pe.wait_ge(max_done, UNITS * (SLOTS // 2) * (m + 1))
                pe.wait_ge(v_done, 2 * (m + 1))
                if late(m, 2):
                    pe.wait_ge(wo_done, 1 + CT * (m - 1))

            def transpose_max(par):
                nc.tensor.transpose(misc[0:H * TT, 0:P], neg_max[par][:, :], ident[:, :]).then_inc(m_ready, 1)

            def weigh_values(tc, u, par, st):
                pe.wait_ge(exp_done, SLOTS * tc + UH * (st + 1))
                if st == 0 and late(tc, 1):
                    pe.wait_ge(o_done, tc)
                for j in range(UH):
                    last = nc.tensor.matmul(o_ps[VW * j:VW * (j + 1), :], v_sb[par][:, st, UH * u + j, :],
                                            probs[:, st, j, :], start=(st == 0), stop=(st == TT - 1),
                                            skip_group_check=True)
                last.then_inc(pv_done, 1)

            def turn_x1n(f):
                if f:
                    pe.wait_ge(logits_done, f)
                for ct in range(CT):
                    pe.wait_ge(x1n_ready, CT * f + ct + 1)
                    for kt in range(KT):
                        last = nc.tensor.transpose(s_ps[ct][:, 0, P * kt:P * (kt + 1)],
                                                   x1n[:, f % 2, ct, P * kt:P * (kt + 1)], ident[:, :])
                    last.then_inc(x1t_ready, 1)

            def router_products(f):
                pe.wait_ge(x1t_done, CT * (f + 1))
                for kt in range(KT):
                    last = nc.tensor.matmul(s_ps[0][WG_COLS * kt:WG_COLS * (kt + 1), 0, 0:C], wg_sb[:, kt, :],
                                            x1t[:, kt, :], start=True, stop=True, skip_group_check=True)
                last.then_inc(logits_t_ready, 1)

            def turn_logits(f):
                pe.wait_ge(logits_t_done, f + 1)
                for ct in range(CT):
                    last = nc.tensor.transpose(s_ps[1][:, 0, P * ct:P * (ct + 1)], logits_t[:, P * ct:P * (ct + 1)],
                                               ident[:, :])
                last.then_inc(logits_ready, 1)

            for name in ("wq", "wk"):
                pe.wait_ge(w_loaded[name], 16)
            for j in range(2 * CT):
                project_qk(0, 0, 0, j)
            for name in ("wo", "wv"):
                pe.wait_ge(w_loaded[name], 16)
            pe.wait_ge(vecs_loaded, 4 * 16)
            for ot in range(CT):
                for ct in range(CT):
                    last = nc.tensor.matmul(misc[:, ot:ot + 1], w_sb["wo"][:, ct, P * ot:P * (ot + 1)],
                                            bv_sb[:, ct:ct + 1], start=(ct == 0), stop=(ct == CT - 1))
            last.then_inc(wo_ready, 1)
            pe.wait_ge(ident_ready, 1)
            pe.wait_ge(wo_done, 1)

            def step(n, par, u, i):
                tc = UNITS * n + u - LAG
                cu, cpar = (u - 1, 1 - par) if u else (UNITS - 1, par)
                if early(n, 7):
                    pe.wait_ge(stack_loaded[u], 16 * STACK_DMAS * (n + 1))
                if isinstance(n, int) and n == 1 and u == 1:
                    pe.wait_ge(const_ready, 4)
                if u == 1 and unit_runs(n, u):
                    pe.wait_ge(m_loaded, 16 * PARTS * n)
                    pe.wait_ge(v_done, 2 * n)
                for slot in range(SLOTS):
                    turns = u == 0 and slot == 2 and late(n, 1) and early(n, 8)
                    if turns:
                        wait_to_transpose(n - 1)
                    if early(n, 7):
                        pair, half = slot // 2, slot % 2
                        if half == 0 and (pair >= 2 or u >= 1 or late(n, 1)):
                            pe.wait_ge(max_done, (SLOTS // 2) * (UNITS * n + u) + pair - 1)
                        h, tt = UH * u + slot // TT, slot % TT
                        last = nc.tensor.matmul(s_ps[pair % 2][:, half, :], qs[par][0:QROWS, h, P * tt:P * (tt + 1)],
                                                ks[par][0:QROWS, h, :], start=True, stop=True)
                        if half == 1:
                            last.then_inc(s_ready, 1)
                    if unit_runs(n, u):
                        if slot >= 2 or late(tc, 1):
                            pe.wait_ge(exp_done, SLOTS * tc + slot - 1)
                        st, h = slot // UH, UH * cu + slot % UH
                        nc.tensor.matmul(st_ps[slot % 2][:, :], ks[cpar][0:KROWS, h, P * st:P * (st + 1)],
                                         qs[cpar][0:KROWS, h, :], start=True, stop=True).then_inc(st_ready, 1)
                    if slot == 3 and unit_runs(n, u - 1):
                        pu, ppar = (cu - 1, cpar) if cu else (UNITS - 1, 1 - cpar)
                        weigh_values(tc - 1, pu, ppar, TT - 1)
                    if slot % UH == UH - 1 and slot > UH and unit_runs(n, u):
                        weigh_values(tc, cu, cpar, slot // UH - 1)
                    if turns:
                        transpose_max(1 - par)
                    if early(n, 6) and u == 0 and slot in (4, 8, 12):
                        project_qk(n + 1, 1 - par, i + par, slot // 4 - 1)
                    if early(n, 6) and u == 1 and slot == 4:
                        project_qk(n + 1, 1 - par, i + par, 3)
                    if early(n, 7) and u == 2 and slot in (4, 10):
                        project_v(n, par, slot // 10)
                    if late(n, 2) and u == 3 and slot in (6, 12):
                        project_out(n - 2, slot // 12)
                    f = routes(n, u)
                    if f is not None:
                        if f == 0 and slot == 5:
                            pe.wait_ge(route_loaded, 32)
                        if slot == 5:
                            turn_x1n(f)
                        if slot == 9:
                            router_products(f)
                        if slot == 13:
                            turn_logits(f)

            iterate(pe, step)
            for stage in (turn_x1n, router_products, turn_logits):
                stage(B - 1)


def experts(nc, x1, route, top_at, xn_stored, x1_stored, xn_rows, w1, w3, w2, out):
    es = ExitStack()
    with es:
        def sb(name, shape, dt):
            return es.enter_context(nc.sbuf_tensor(name, shape, dt))

        def ps(name, shape):
            return es.enter_context(nc.psum_tensor(name, shape, F32))

        def sem(name):
            return es.enter_context(nc.semaphore(name))

        w13_raw = [sb(f"w13_raw{i}", [P, KT, 2 * FF], F32) for i in range(2)]
        w2_raw = [sb(f"w2_raw{i}", [P, FT, T], F32) for i in range(2)]
        w13_hi = [sb(f"w13_hi{i}", [P, KT, 2 * FF], F32R) for i in range(2)]
        w13_lo = [sb(f"w13_lo{i}", [P, KT, 2 * FF], F32R) for i in range(2)]
        w2_hi = [sb(f"w2_hi{i}", [P, FT, T], F32R) for i in range(2)]
        w2_lo = [sb(f"w2_lo{i}", [P, FT, T], F32R) for i in range(2)]
        ident = sb("ident2", [P, P], F32)
        pause = sb("pause", [P, 3], F32)
        zero = sb("zero", [P, 1], F32)
        lanes = sb("lanes", [P, P], F32)
        token_1 = sb("token_1", [P, TILES], F32)
        below = sb("below", [P, P], BF16)
        ones = sb("ones", [P, P], BF16)
        top_lane = sb("top_lane", [P, TOP, TILES], F32)
        chosen = sb("chosen", [P, TOP, TILES, E], F32)
        mask = sb("mask", [P, 2 * TILES + 1, E], BF16)
        picked = sb("picked", [P, TOP, TILES, E], F32)
        top_route = sb("top_route", [P, TOP, TILES], F32)
        total = sb("total", [P, TILES], F32)
        rtotal = sb("rtotal", [P, TILES], F32)
        weight = sb("weight", [P, TOP, TILES], F32)
        weight_hi = sb("weight_hi", [P, TOP, TILES], F32R)
        weight_lo = sb("weight_lo", [P, TOP, TILES], F32)
        rounded = sb("rounded", [P, E], U32)
        blocks_i = sb("blocks_i", [P, E], U32)
        blocks_f = sb("blocks_f", [P, E], F32)
        sums = [sb(f"sums{i}", [P, E // 2 + 1 + E], F32) for i in range(4)]
        start = sums[3][:, E // 2:E // 2 + 1 + E]
        spans = sb("spans", [P, E + 2], mybir.dt.int32)
        place = sb("place", [P, TILES, E], F32)
        slot_f = sb("slot_f", [P, TOP * TILES], F32)
        slot_i = sb("slot_i", [P, TOP * TILES], U32)
        row_i = sb("row_i", [P, TOP * TILES], U32)
        block_i = sb("block_i", [P, TOP * TILES], U32)
        row_f = sb("row_f", [P, TOP * TILES], F32)
        block_f = sb("block_f", [P, TOP * TILES], F32)
        row_hot = sb("row_hot", [P, TOP * TILES, P], F32R)
        block_hot = sb("block_hot", [P, TOP * TILES, BLOCKS], F32)
        entries = sb("entries", [P, TOP * TILES, PLANES, BLOCKS], F32R)
        weight_part = sb("weight_part", [P, BLOCKS], F32)
        empty = sb("empty", [P, BLOCKS], F32)
        ids = sb("ids", [P, 2 * TABLE], U32)
        block_weight = sb("block_weight", [P, 2 * TABLE], F32)
        id_in = sb("id_in", [P, 1], U32)
        id_out = sb("id_out", [P, 1], U32)
        rows = sb("rows", [P, T], F32)
        xb_hi = sb("xb_hi", [P, KT, P], F32R)
        xb_lo = sb("xb_lo", [P, KT, P], F32R)
        silu = sb("silu", [P, FF], F32)
        g = sb("g", [P, FF], F32)
        gt_hi = sb("gt_hi", [P, FT, P], F32R)
        gt_lo = sb("gt_lo", [P, FT, P], F32R)
        y_sb = sb("y_sb", [P, T], F32)

        t_ps = ps("t_ps", [P, T])
        h_ps = ps("h_ps", [P, T])
        y_ps = ps("y_ps", [P, T])
        gt_ps = ps("gt_ps", [P, FT, P])
        rank_ps = ps("rank_ps", [P, TILES + 1, E])
        table_ps = ps("table_ps", [P, PLANES, BLOCKS])

        raw_loaded = [sem(f"raw_loaded{i}") for i in range(2)]
        ident_zero, consts, below_ones, sums_zero = sem("ident_zero2"), sem("consts"), sem("below_ones"), sem("sums_zero")
        rows_zero, ids_empty = sem("rows_zero"), sem("ids_empty")
        chain, mask_ready, rank_ready = sem("chain"), sem("mask_ready"), sem("rank_ready")
        blocks_hot, tokens_entered, weights_entered, rows_hot = (
            sem(n) for n in ("blocks_hot", "tokens_entered", "weights_entered", "rows_hot"))
        spans_ready, table_summed, table_ready = sem("spans_ready"), sem("table_summed"), sem("table_ready")
        w13_hi_cut, w13_cut, w2_hi_cut, w2_cut = (sem(n) for n in ("w13_hi_cut", "w13_cut", "w2_hi_cut", "w2_cut"))
        id_in_ready, id_out_ready, gathered = sem("id_in_ready"), sem("id_out_ready"), sem("gathered")
        t_ready, xb_hi_done, xb_done = sem("t_ready"), sem("xb_hi_done"), sem("xb_done")
        h_ready, silu_done, g_done = sem("h_ready"), sem("silu_done"), sem("g_done")
        gt_ready, gt_hi_done, gt_done = sem("gt_ready"), sem("gt_hi_done"), sem("gt_done")
        y_ready, y_done = sem("y_ready"), sem("y_done")
        out_written = sem("out_written")

        out_rows = out.rearrange("n c t -> (n c) t")
        in_rows = xn_rows.rearrange("n c t -> (n c) t")

        def f32(ap):
            return ap.bitcast(F32)

        def load_start(engine, e):
            return engine.value_load(spans[0:1, bass.ds(e, 1)], min_val=0, max_val=BLOCKS)

        def load_tail(engine):
            return engine.value_load(spans[0:1, E + 1:E + 2], min_val=MIN_BLOCKS * E - 2, max_val=BLOCKS - 2)

        def over_blocks(engine, block):
            def pair(i, is_first, is_last):
                first = load_start(engine, 2 * i)
                for par in range(2):
                    e = 2 * i + par
                    has_next = not (is_last and par == 1)
                    opening = is_first and par == 0
                    block(0 if opening else first, e, par, True, not opening, has_next)
                    following = load_start(engine, e + 1)
                    with engine.If(first + 1 < following):
                        with engine.Fori(first + 1, following) as b:
                            block(b, e, par, False, True, has_next)
                    first = following

            pair(0, True, False)
            with engine.Fori(1, E // 2 - 1) as i:
                pair(i, False, False)
            pair(E // 2 - 1, False, True)

        block = es.enter_context(nc.Block())

        @block.sync
        def _(sp):
            def load(e, par):
                sp.dma_start(w13_raw[par][:, :, 0:FF], w1[bass.ds(e, 1)].rearrange("o (k p) f -> p (o k) f", p=P)
                             ).then_inc(raw_loaded[par], 16)
                sp.dma_start(w13_raw[par][:, :, FF:2 * FF], w3[bass.ds(e, 1)].rearrange("o (k p) f -> p (o k) f", p=P)
                             ).then_inc(raw_loaded[par], 16)
                sp.dma_start(w2_raw[par][:, :, :], w2[bass.ds(e, 1)].rearrange("o (k p) t -> p (o k) t", p=P)
                             ).then_inc(raw_loaded[par], 16)

            load(0, 0)
            load(1, 1)
            with sp.Fori(1, E // 2) as i:
                for par in range(2):
                    sp.wait_ge(w13_cut, 2 * (2 * i + par - 1))
                    sp.wait_ge(w2_cut, 2 * i + par - 1)
                    load(2 * i + par, par)

        @block.gpsimd
        def _(pool):
            nc.gpsimd.iota(lanes[:, :], pattern=[[1, P]], base=0, channel_multiplier=0,
                           allow_small_or_imprecise_dtypes=True).then_inc(consts, 1)
            nc.gpsimd.memset(ones[:, :], 1.0)
            nc.gpsimd.memset(below[:, :], 1.0).then_inc(below_ones, 1)
            pool.wait_ge(below_ones, 1)
            nc.gpsimd.affine_select(out=below[:, :], in_=below[:, :], compare_op=ALU.is_gt, fill=0.0, base=0,
                                    pattern=[[1, P]], channel_multiplier=-1).then_inc(consts, 1)
            nc.gpsimd.iota(token_1[:, :], pattern=[[P, TILES]], base=1, channel_multiplier=1,
                           allow_small_or_imprecise_dtypes=True).then_inc(consts, 1)
            nc.gpsimd.memset(ident[:, :], 0.0).then_inc(ident_zero, 1)
            pool.wait_ge(ident_zero, 1)
            nc.gpsimd.affine_select(out=ident[:, :], in_=ident[:, :], compare_op=ALU.not_equal, fill=1.0, base=0,
                                    pattern=[[-1, P]], channel_multiplier=1).then_inc(consts, 1)
            nc.gpsimd.dma_start(out[B - 1].rearrange("(c p) t -> p c t", p=P), x1[:, B - 1, :, :]
                                ).then_inc(out_written, 16)
            nc.gpsimd.memset(zero[:, :], 0.0)
            nc.gpsimd.memset(rows[:, :], 0.0).then_inc(rows_zero, 1)
            nc.gpsimd.memset(ids[:, BLOCKS:TABLE], 2 * TOKENS - 1).then_inc(ids_empty, 1)
            pool.wait_ge(blocks_hot, 1)
            for chunk in range(CHUNKS):
                js = slice(CHUNK * chunk, CHUNK * (chunk + 1))
                i0 = CHUNK * chunk % TILES
                nc.gpsimd.tensor_tensor(entries[:, js, 0, :], block_hot[:, js, :],
                                        token_1[:, i0:i0 + CHUNK].rearrange("p (i o) -> p i o", o=1).to_broadcast(
                                            [P, CHUNK, BLOCKS]), ALU.mult).then_inc(tokens_entered, 1)

            def gather(b):
                nc.gpsimd.tensor_copy(id_in[:, :], ids[:, bass.ds(b, 1)]).then_inc(id_in_ready, 1)
                pool.wait_ge(id_in_ready, b + 1)
                nc.gpsimd.tensor_tensor(pause[:, 0:1], zero[:, :], zero[:, :], ALU.add)
                for stored in xn_stored:
                    pool.wait_ge(stored, 16 * (B // 2))
                nc.gpsimd.indirect_dma_start(rows[:, :], None, in_rows,
                                             bass.IndirectOffsetOnAxis(ap=id_in[:, 0:1], axis=0),
                                             bounds_check=TOKENS - 1, oob_is_err=False).then_inc(gathered, 16)

            def scatter(b):
                pool.wait_ge(out_written, 16 * (b + 1))
                nc.gpsimd.tensor_copy(id_out[:, :], ids[:, bass.ds(b, 1)]).then_inc(id_out_ready, 1)
                pool.wait_ge(y_done, b + 1)
                pool.wait_ge(id_out_ready, b + 1)
                nc.gpsimd.tensor_tensor(pause[:, 1:2], zero[:, :], zero[:, :], ALU.add)
                nc.gpsimd.indirect_dma_start(out_rows, bass.IndirectOffsetOnAxis(ap=id_out[:, 0:1], axis=0),
                                             y_sb[:, :], None, bounds_check=TOKENS - 1, oob_is_err=False,
                                             compute_op=ALU.add).then_inc(out_written, 16)

            pool.wait_ge(spans_ready, 2)
            pool.wait_ge(table_ready, 1)
            pool.wait_ge(rows_zero, 1)
            pool.wait_ge(x1_stored, 16 * (B - 1))
            tail = load_tail(pool)
            gather(0)
            for b in (0, 1):
                pool.wait_ge(t_ready, b + 1)
                gather(b + 1)
            with pool.Fori(0, tail) as b:
                pool.wait_ge(t_ready, b + 3)
                gather(b + 3)
                scatter(b)
            scatter(tail)
            scatter(tail + 1)
            pool.wait_ge(out_written, 16 * (tail + 3))
            nc.gpsimd.tensor_tensor(pause[:, 2:3], zero[:, :], zero[:, :], ALU.add)

        @block.scalar
        def _(act):
            def cut_w13(e, par, half):
                kts = slice(KT // 2 * half, KT // 2 * (half + 1))
                if half == 0:
                    act.wait_ge(raw_loaded[par], 24 * (e - par) + 48)
                nc.scalar.copy(w13_hi[par][:, kts, :], w13_raw[par][:, kts, :]).then_inc(w13_hi_cut, 1)

            def cut_w2(e, par):
                nc.scalar.copy(w2_hi[par][:, :, :], w2_raw[par][:, :, :]).then_inc(w2_hi_cut, 1)

            cut_w13(0, 0, 0)
            cut_w13(0, 0, 1)
            cut_w2(0, 0)

            act.wait_ge(spans_ready, 2)

            def split_rows(b):
                act.wait_ge(t_ready, b + 1)
                nc.scalar.copy(xb_hi[:, :, :], t_ps[:, :].rearrange("p (k t) -> p k t", k=KT)
                               ).then_inc(xb_hi_done, 1)

            def take_y(b):
                act.wait_ge(out_written, 16 * (b + 1))
                act.wait_ge(y_ready, b + 1)
                nc.scalar.copy(y_sb[:, :], y_ps[:, :]).then_inc(y_done, 1)

            def step(b, e, par, opens, started, has_next):
                act.wait_ge(h_ready, b + 1)
                nc.scalar.activation(silu[:, :], h_ps[:, 0:FF], ACT.Silu).then_inc(silu_done, 1)
                split_rows(b + 1)
                if opens and has_next:
                    cut_w13(e + 1, 1 - par, 0)
                if started:
                    take_y(b - 1)
                act.wait_ge(gt_ready, b + 1)
                nc.scalar.copy(gt_hi[:, :, :], gt_ps[:, :, :]).then_inc(gt_hi_done, 1)
                if opens and has_next:
                    cut_w13(e + 1, 1 - par, 1)
                    cut_w2(e + 1, 1 - par)

            split_rows(0)
            over_blocks(act, step)
            take_y(load_tail(act) + 1)

        @block.vector
        def _(dve):
            def cut_w13(e, par, half):
                kts = slice(KT // 2 * half, KT // 2 * (half + 1))
                dve.wait_ge(w13_hi_cut, 2 * e + half + 1)
                nc.vector.tensor_tensor(w13_lo[par][:, kts, :], w13_raw[par][:, kts, :], f32(w13_hi[par][:, kts, :]),
                                        ALU.subtract).then_inc(w13_cut, 1)

            def cut_w2(e, par):
                dve.wait_ge(w2_hi_cut, e + 1)
                nc.vector.tensor_tensor(w2_lo[par][:, :, :], w2_raw[par][:, :, :], f32(w2_hi[par][:, :, :]),
                                        ALU.subtract).then_inc(w2_cut, 1)

            nc.vector.memset(mask[:, 0:TILES, :], 0.0).then_inc(mask_ready, 1)
            nc.vector.memset(mask[:, 2 * TILES, :], 0.0).then_inc(mask_ready, 1)
            for i in range(4):
                nc.vector.memset(sums[i][:, 0:E // 2 + 1], 0.0).then_inc(sums_zero, 1)
            count = [0]

            def link(instruction):
                count[0] += 1
                instruction.then_inc(chain, 1)
                dve.wait_ge(chain, count[0])

            def spread(ap, shape):
                return ap.to_broadcast(shape)

            every = [P, TILES, E]
            both = [P, TOP, TILES, E]
            dve.wait_ge(consts, 1)
            link(nc.vector.tensor_copy(top_lane[:, :, :], top_at[:, :, 0:TOP].rearrange("p i k -> p k i")))
            link(nc.vector.tensor_tensor(
                chosen[:, :, :, :].rearrange("p k i e -> p (k i) e"),
                spread(lanes[:, 0:E].rearrange("p (o e) -> p o e", o=1), [P, TOP * TILES, E]),
                spread(top_lane[:, :, :].rearrange("p k (i o) -> p (k i) o", o=1), [P, TOP * TILES, E]), ALU.is_equal))
            nc.vector.tensor_tensor(mask[:, TILES:2 * TILES, :], chosen[:, 0, :, :], chosen[:, 1, :, :], ALU.add
                                    ).then_inc(mask_ready, 1)
            for k in range(TOP):
                nc.vector.tensor_tensor(picked[:, k, :, :], chosen[:, k, :, :], route[:, :, :],
                                        ALU.mult).then_inc(chain, 1)
            count[0] += TOP
            dve.wait_ge(chain, count[0])
            link(nc.vector.tensor_reduce(top_route[:, :, :].rearrange("p k i -> p (k i)"),
                                         picked[:, :, :, :].rearrange("p k i e -> p (k i) e"), AX.X, ALU.add))
            link(nc.vector.tensor_tensor(total[:, :], top_route[:, 0, :], top_route[:, 1, :], ALU.add))
            link(nc.vector.reciprocal(rtotal[:, :], total[:, :]))
            link(nc.vector.tensor_tensor(weight[:, :, :], top_route[:, :, :],
                                         spread(rtotal[:, :].rearrange("p (o i) -> p o i", o=1), [P, TOP, TILES]),
                                         ALU.mult))
            link(nc.vector.tensor_copy(weight_hi[:, :, :], weight[:, :, :]))
            link(nc.vector.tensor_tensor(weight_lo[:, :, :], weight[:, :, :], f32(weight_hi[:, :, :]), ALU.subtract))
            dve.wait_ge(rank_ready, 1)
            link(nc.vector.tensor_scalar(rounded[:, :], rank_ps[:, TILES, :], float(P - 1), None, ALU.add))
            link(nc.vector.tensor_scalar(blocks_i[:, :], rounded[:, :], SHIFT, None, ALU.logical_shift_right))
            link(nc.vector.tensor_scalar(blocks_f[:, :], blocks_i[:, :], float(MIN_BLOCKS), None, ALU.max))
            dve.wait_ge(sums_zero, 4)
            ahead = E // 2 + 1
            link(nc.vector.tensor_copy(sums[0][:, ahead:ahead + E], blocks_f[:, :]))
            for i in range(3):
                back = 1 << i
                link(nc.vector.tensor_tensor(sums[i + 1][:, ahead:ahead + E], sums[i][:, ahead:ahead + E],
                                             sums[i][:, ahead - back:ahead + E - back], ALU.add))
            nc.vector.tensor_copy(spans[:, 0:E + 1], start).then_inc(spans_ready, 1)
            nc.vector.tensor_scalar(spans[:, E + 1:E + 2], start[:, E:E + 1], -2.0, None, ALU.add).then_inc(spans_ready, 1)
            link(nc.vector.scalar_tensor_tensor(
                out=place[:, :, :], in0=spread(start[:, 0:E].rearrange("p (o e) -> p o e", o=1), every),
                scalar=float(P), in1=rank_ps[:, 0:TILES, :], op0=ALU.mult, op1=ALU.add))
            for k in range(TOP):
                nc.vector.tensor_tensor(picked[:, k, :, :], chosen[:, k, :, :], place[:, :, :],
                                        ALU.mult).then_inc(chain, 1)
            count[0] += TOP
            dve.wait_ge(chain, count[0])
            link(nc.vector.tensor_reduce(slot_f[:, :], picked[:, :, :, :].rearrange("p k i e -> p (k i) e"),
                                         AX.X, ALU.add))
            link(nc.vector.tensor_copy(slot_i[:, :], slot_f[:, :]))
            link(nc.vector.tensor_scalar(block_i[:, :], slot_i[:, :], SHIFT, None, ALU.logical_shift_right))
            link(nc.vector.tensor_scalar(row_i[:, :], slot_i[:, :], P - 1, None, ALU.bitwise_and))
            link(nc.vector.tensor_copy(block_f[:, :], block_i[:, :]))
            link(nc.vector.tensor_copy(row_f[:, :], row_i[:, :]))
            hot = [P, TOP * TILES, BLOCKS]
            nc.vector.tensor_tensor(block_hot[:, :, :], spread(lanes[:, 0:BLOCKS].rearrange("p (o b) -> p o b", o=1), hot),
                                    spread(block_f[:, :].rearrange("p (j o) -> p j o", o=1), hot), ALU.is_equal
                                    ).then_inc(blocks_hot, 1)
            dve.wait_ge(blocks_hot, 1)
            for chunk in range(CHUNKS):
                js = slice(CHUNK * chunk, CHUNK * (chunk + 1))
                for plane, part in ((1, f32(weight_hi[:, :, :])), (2, weight_lo[:, :, :])):
                    nc.vector.tensor_tensor(entries[:, js, plane, :], block_hot[:, js, :],
                                            spread(part.rearrange("p k (i o) -> p (k i) o", o=1)[:, js, :],
                                                   [P, CHUNK, BLOCKS]), ALU.mult).then_inc(weights_entered, 1)
                hot = [P, CHUNK, P]
                nc.vector.tensor_tensor(row_hot[:, js, :], spread(lanes[:, :].rearrange("p (o b) -> p o b", o=1), hot),
                                        spread(row_f[:, js].rearrange("p (j o) -> p j o", o=1), hot),
                                        ALU.is_equal).then_inc(rows_hot, 1)
            dve.wait_ge(table_summed, 1)
            link(nc.vector.tensor_scalar(empty[:, :], table_ps[:, 0, :], 0.0, float(2 * TOKENS),
                                         ALU.is_equal, ALU.mult))
            nc.vector.scalar_tensor_tensor(out=ids[:, 0:BLOCKS], in0=empty[:, :], scalar=-1.0, in1=table_ps[:, 0, :],
                                           op0=ALU.add, op1=ALU.add).then_inc(table_ready, 1)
            link(nc.vector.tensor_copy(weight_part[:, :], table_ps[:, 2, :]))
            link(nc.vector.tensor_tensor(block_weight[:, 0:BLOCKS], weight_part[:, :], table_ps[:, 1, :], ALU.add))
            cut_w13(0, 0, 0)
            cut_w13(0, 0, 1)
            cut_w2(0, 0)
            dve.wait_ge(spans_ready, 2)

            def split_rows(b):
                dve.wait_ge(xb_hi_done, b + 1)
                nc.vector.tensor_tensor(xb_lo[:, :, :], t_ps[:, :].rearrange("p (k t) -> p k t", k=KT),
                                        f32(xb_hi[:, :, :]), ALU.subtract).then_inc(xb_done, 1)

            def step(b, e, par, opens, started, has_next):
                dve.wait_ge(silu_done, b + 1)
                nc.vector.scalar_tensor_tensor(out=g[:, :], in0=silu[:, :], scalar=block_weight[:, bass.ds(b, 1)],
                                               in1=h_ps[:, FF:2 * FF], op0=ALU.mult, op1=ALU.mult).then_inc(g_done, 1)
                split_rows(b + 1)
                if opens and has_next:
                    cut_w13(e + 1, 1 - par, 0)
                dve.wait_ge(gt_hi_done, b + 1)
                nc.vector.tensor_tensor(gt_lo[:, :, :], gt_ps[:, :, :], f32(gt_hi[:, :, :]),
                                        ALU.subtract).then_inc(gt_done, 1)
                if opens and has_next:
                    cut_w13(e + 1, 1 - par, 1)
                    cut_w2(e + 1, 1 - par)

            split_rows(0)
            over_blocks(dve, step)

        @block.tensor
        def _(pe):
            pe.wait_ge(consts, 2)
            pe.wait_ge(mask_ready, 3)
            for back in range(TILES + 1):
                last = nc.tensor.matmul(rank_ps[:, :, :], ones[:, :] if back else below[:, :],
                                        mask[:, TILES - back:2 * TILES + 1 - back, :],
                                        start=(back == 0), stop=(back == TILES))
            last.then_inc(rank_ready, 1)
            for j in range(TOP * TILES):
                if j % CHUNK == 0:
                    pe.wait_ge(tokens_entered, j // CHUNK + 1)
                    pe.wait_ge(weights_entered, 2 * (j // CHUNK + 1))
                    pe.wait_ge(rows_hot, j // CHUNK + 1)
                last = nc.tensor.matmul(table_ps[:, :, :].rearrange("p w b -> p (w b)"), row_hot[:, j, :],
                                        entries[:, j, :, :].rearrange("p w b -> p (w b)"),
                                        start=(j == 0), stop=(j == TOP * TILES - 1))
            last.then_inc(table_summed, 1)

            pe.wait_ge(consts, 4)

            def turn_rows(b):
                pe.wait_ge(gathered, 16 * (b + 1))
                for kt in range(KT):
                    last = nc.tensor.transpose(t_ps[:, P * kt:P * (kt + 1)], rows[:, P * kt:P * (kt + 1)],
                                               ident[:, :])
                last.then_inc(t_ready, 1)

            def down(b, par):
                pe.wait_ge(gt_done, b + 1)
                for ft in range(FT):
                    for gt, w in ((gt_hi, w2_hi), (gt_hi, w2_lo), (gt_lo, w2_hi)):
                        last = nc.tensor.matmul(y_ps[:, :], gt[:, ft, :], w[par][:, ft, :],
                                                start=(ft == 0 and gt is gt_hi and w is w2_hi),
                                                stop=(ft == FT - 1 and gt is gt_lo))
                last.then_inc(y_ready, 1)

            def step(b, e, par, opens, started, has_next):
                pe.wait_ge(xb_done, b + 1)
                for kt in range(KT):
                    if opens and kt % (KT // 2) == 0:
                        pe.wait_ge(w13_cut, 2 * e + 1 + kt // (KT // 2))
                    for x, w in ((xb_hi, w13_hi), (xb_hi, w13_lo), (xb_lo, w13_hi)):
                        last = nc.tensor.matmul(h_ps[:, :], x[:, kt, :], w[par][:, kt, :],
                                                start=(kt == 0 and x is xb_hi and w is w13_hi),
                                                stop=(kt == KT - 1 and x is xb_lo))
                last.then_inc(h_ready, 1)
                turn_rows(b + 1)
                if started:
                    down(b - 1, 1 - par if opens else par)
                if opens:
                    pe.wait_ge(w2_cut, e + 1)
                pe.wait_ge(g_done, b + 1)
                for ft in range(FT):
                    last = nc.tensor.transpose(gt_ps[:, ft, :], g[:, P * ft:P * (ft + 1)], ident[:, :])
                last.then_inc(gt_ready, 1)

            pe.wait_ge(spans_ready, 2)
            turn_rows(0)
            over_blocks(pe, step)
            down(load_tail(pe) + 1, 1)


def xattn_moe(nc, x, ctx_in, wq, bq, wk, bk, wv, bv, wo, bo, wg, w1, w3, w2, bias, out):
    q_scratch = nc.dram_tensor("q_scratch", [B, 2, PARTS, HD, H, T], BF16, kind="Internal").ap()
    o_scratch = nc.dram_tensor("o_scratch", [B, UNITS, P, T], F32, kind="Internal").ap()
    r_scratch = nc.dram_tensor("r_scratch", [B, H, T], F32, kind="Internal").ap()
    xn_rows = nc.dram_tensor("xn_rows", [B, C, T], F32, kind="Internal").ap()
    with (nc.sbuf_tensor("x1", [P, B, CT, T], F32) as x1, nc.sbuf_tensor("route", [P, TILES, E], F32) as route,
          nc.sbuf_tensor("top_at", [P, TILES, E], U32) as top_at,
          nc.semaphore("xn_stored0") as xn_stored0, nc.semaphore("xn_stored1") as xn_stored1,
          nc.semaphore("x1_stored") as x1_stored):
        xn_stored = (xn_stored0, xn_stored1)
        attention(nc, x, ctx_in, wq, bq, wk, bk, wv, bv, wo, bo, wg, bias, x1, route, top_at, xn_stored, x1_stored,
                  q_scratch, o_scratch, r_scratch, xn_rows, out)
        experts(nc, x1, route, top_at, xn_stored, x1_stored, xn_rows, w1, w3, w2, out)


def kernel(x, ctx_2048, L0_xattn_Wq, L0_xattn_bq, L0_xattn_Wk, L0_xattn_bk, L0_xattn_Wv, L0_xattn_bv,
           L0_xattn_Wo, L0_xattn_bo, L0_ffn_Wg, L0_ffn_W1, L0_ffn_W2, L0_ffn_W3, L0_ffn_bias):
    import numpy as np
    import concourse.bacc as bacc
    from concourse.bass_utils import run_bass_kernel_spmd

    def by_channel(w):
        w = np.asarray(w)
        return np.swapaxes(w.reshape(H, HD, *w.shape[1:]), 0, 1).reshape(w.shape)

    def column(v):
        return np.asarray(v).reshape(CT, P).T

    arrays = {
        "x": x, "ctx": ctx_2048,
        "wq": by_channel(L0_xattn_Wq).T, "bq": column(by_channel(L0_xattn_bq)),
        "wk": by_channel(L0_xattn_Wk).T, "bk": column(by_channel(L0_xattn_bk)),
        "wv": np.asarray(L0_xattn_Wv).T, "bv": column(L0_xattn_bv),
        "wo": np.asarray(L0_xattn_Wo).T, "bo": column(L0_xattn_bo),
        "wg": np.asarray(L0_ffn_Wg).T,
        "w1": np.swapaxes(np.asarray(L0_ffn_W1), 1, 2), "w3": np.swapaxes(np.asarray(L0_ffn_W3), 1, 2),
        "w2": np.swapaxes(np.asarray(L0_ffn_W2), 1, 2), "bias": np.asarray(L0_ffn_bias).reshape(1, E),
    }
    arrays = {f"in_{k}": np.ascontiguousarray(v) for k, v in arrays.items()}
    nc = bacc.Bacc("TRN2", target_bir_lowering=False, num_devices=1)
    args = [nc.dram_tensor(k, v.shape, mybir.dt.from_np(v.dtype), kind="ExternalInput").ap() for k, v in arrays.items()]
    out = nc.dram_tensor("out", [B, C, T], F32, kind="ExternalOutput").ap()
    xattn_moe(nc, *args, out)
    return run_bass_kernel_spmd(nc, [arrays], core_ids=[0]).results[0]["out"]
```
